# Optimizing a Trainium2 kernel written in Bass

```python
import numpy as np
import jax
import jax.numpy as jnp

def _softmax(x, axis=-1):
    return jax.nn.softmax(x, axis=axis)

def _gelu(x):
    return jax.nn.gelu(x, approximate=True)

def _silu(x):
    return jax.nn.silu(x)

def _sigmoid(x):
    return jax.nn.sigmoid(x)

def _layernorm(x, axis=-1, eps=1e-05):
    m = jnp.mean(x, axis=axis, keepdims=True)
    v = jnp.var(x, axis=axis, keepdims=True)
    return (x - m) / jnp.sqrt(v + eps)

def _scatter_add(tgt, idx, src, axis=0):
    return tgt.at[idx].add(src)

def _segment_sum(src, seg, n):
    return jax.ops.segment_sum(src, seg, n)
kernel_name = 'mk_flamingo_gated_d1_seqx_r4_ca9f71'

def setup_inputs(seed: int=0):
    np.random.seed(seed)
    _w = jnp.asarray

    def _rec_inputs():
        import jax
        import jax.numpy as jnp
        _rk = jax.random.key(seed)
        x = -0.0002928 + 1 * jax.random.normal(jax.random.fold_in(_rk, 1), (4, 512, 256), jnp.float32)
        _lenS = 512 - jax.random.randint(jax.random.fold_in(_rk, 7), (4,), 0, max(1, 512 // 4) + 1, jnp.int32)
        _lenS2 = 1601 - jax.random.randint(jax.random.fold_in(_rk, 8), (4,), 0, max(1, 1601 // 4) + 1, jnp.int32)
        _ctx_512P = jax.random.normal(jax.random.fold_in(_rk, 11), (4, 16, 128), jnp.float32)
        _ctx_512c = jax.random.dirichlet(jax.random.fold_in(_rk, 511), 0.3 * jnp.ones((16,), jnp.float32), (4, 1601))
        _ctx_512t = jnp.einsum('bsk,bkd->bsd', _ctx_512c, _ctx_512P)
        _ctx_512t = _ctx_512t * jax.lax.rsqrt(jnp.mean(jnp.square(_ctx_512t)) + 1e-12) * 0.953939
        ctx_512 = 0.00222621 + 0.99962 * (_ctx_512t + 0.3 * jax.random.normal(jax.random.fold_in(_rk, 611), (4, 1601, 128), jnp.float32))
        _g = jax.random.normal(jax.random.fold_in(_rk, 9001), (2, 1), jnp.float32)
        _g = jnp.sign(_g) * jnp.maximum(jnp.abs(_g), 1.0) + (_g == 0) * 1.0
        g_xattn = _g[0]
        g_ffn = _g[1]
        return (x, ctx_512, g_xattn, g_ffn)
    x, ctx_512, g_xattn, g_ffn = _rec_inputs()

    def _L0_xattn_setup():
        import jax, jax.numpy as jnp
        import numpy as np
        B, T, TC, C, CC, H = (2, 512, 128, 256, 128, 16)
        D = C // H

        def _heads(t):
            b, l, _ = t.shape
            return t.reshape(b, l, H, D).transpose(0, 2, 1, 3)
        key = jax.random.key(seed)
        ks = jax.random.split(key, 18)
        w = lambda k, i, o: jax.random.normal(k, (i, o), jnp.float32) / np.sqrt(i).astype(np.float32)
        return {'x': jax.random.normal(ks[0], (B, T, C), jnp.float32), 'cross_input': jax.random.normal(ks[1], (B, TC, CC), jnp.float32), 'Wk': w(ks[2], C, C), 'bk': jnp.zeros((C,), jnp.float32), 'Wq': w(ks[3], C, C), 'bq': jnp.zeros((C,), jnp.float32), 'Wv': w(ks[4], C, C), 'bv': jnp.zeros((C,), jnp.float32), 'Wck': w(ks[5], CC, C), 'bck': jnp.zeros((C,), jnp.float32), 'Wcq': w(ks[6], C, C), 'bcq': jnp.zeros((C,), jnp.float32), 'Wcv': w(ks[7], CC, C), 'bcv': jnp.zeros((C,), jnp.float32), 'Wp': w(ks[8], C, C), 'bp': jnp.zeros((C,), jnp.float32)}
    _L0_xattn_all = _L0_xattn_setup()
    _L0_xattn_in = {k: v for k, v in _L0_xattn_all.items() if k in ('Wk', 'bk', 'Wq', 'bq', 'Wv', 'bv', 'Wck', 'bck', 'Wcq', 'bcq', 'Wcv', 'bcv', 'Wp', 'bp')}
    del _L0_xattn_all

    def _L0_ffn_setup():
        import jax, jax.numpy as jnp
        import numpy as np
        H, I, E_ROUTED, TOP_K = (256, 704, 7, 2)
        B, S = (4, 512)

        def _expert(h, g, u, d):
            return jnp.einsum('...i,hi->...h', jax.nn.silu(h @ g.T) * (h @ u.T), d)
        key = jax.random.key(seed)
        ks = jax.random.split(key, 10)
        sc = 0.02
        return {'x': jax.random.normal(ks[0], (B, S, H), dtype=jnp.float32), 'sg': jax.random.normal(ks[1], (I, H), dtype=jnp.float32) * sc, 'su': jax.random.normal(ks[2], (I, H), dtype=jnp.float32) * sc, 'sd': jax.random.normal(ks[3], (H, I), dtype=jnp.float32) * sc, 'rg': jax.random.normal(ks[4], (E_ROUTED, I, H), dtype=jnp.float32) * sc, 'ru': jax.random.normal(ks[5], (E_ROUTED, I, H), dtype=jnp.float32) * sc, 'rd': jax.random.normal(ks[6], (E_ROUTED, H, I), dtype=jnp.float32) * sc, 'wr': jax.random.normal(ks[7], (E_ROUTED, H), dtype=jnp.float32) * sc, 'rb': jnp.zeros((E_ROUTED,), dtype=jnp.float32)}
    _L0_ffn_all = _L0_ffn_setup()
    _L0_ffn_in = {k: v for k, v in _L0_ffn_all.items() if k in ('sg', 'su', 'sd', 'rg', 'ru', 'rd', 'wr', 'rb')}
    del _L0_ffn_all
    return {'x': x, 'ctx_512': ctx_512, 'g_xattn': g_xattn, 'g_ffn': g_ffn, 'L0_xattn_Wk': _L0_xattn_in['Wk'], 'L0_xattn_bk': _L0_xattn_in['bk'], 'L0_xattn_Wq': _L0_xattn_in['Wq'], 'L0_xattn_bq': _L0_xattn_in['bq'], 'L0_xattn_Wv': _L0_xattn_in['Wv'], 'L0_xattn_bv': _L0_xattn_in['bv'], 'L0_xattn_Wck': _L0_xattn_in['Wck'], 'L0_xattn_bck': _L0_xattn_in['bck'], 'L0_xattn_Wcq': _L0_xattn_in['Wcq'], 'L0_xattn_bcq': _L0_xattn_in['bcq'], 'L0_xattn_Wcv': _L0_xattn_in['Wcv'], 'L0_xattn_bcv': _L0_xattn_in['bcv'], 'L0_xattn_Wp': _L0_xattn_in['Wp'], 'L0_xattn_bp': _L0_xattn_in['bp'], 'L0_ffn_sg': _L0_ffn_in['sg'], 'L0_ffn_su': _L0_ffn_in['su'], 'L0_ffn_sd': _L0_ffn_in['sd'], 'L0_ffn_rg': _L0_ffn_in['rg'], 'L0_ffn_ru': _L0_ffn_in['ru'], 'L0_ffn_rd': _L0_ffn_in['rd'], 'L0_ffn_wr': _L0_ffn_in['wr'], 'L0_ffn_rb': _L0_ffn_in['rb']}

def reference(x, ctx_512, g_xattn, g_ffn, L0_xattn_Wk, L0_xattn_bk, L0_xattn_Wq, L0_xattn_bq, L0_xattn_Wv, L0_xattn_bv, L0_xattn_Wck, L0_xattn_bck, L0_xattn_Wcq, L0_xattn_bcq, L0_xattn_Wcv, L0_xattn_bcv, L0_xattn_Wp, L0_xattn_bp, L0_ffn_sg, L0_ffn_su, L0_ffn_sd, L0_ffn_rg, L0_ffn_ru, L0_ffn_rd, L0_ffn_wr, L0_ffn_rb):
    import jax
    import jax.numpy as jnp

    def _L0_xattn_ref(x, cross_input, Wk, bk, Wq, bq, Wv, bv, Wck, bck, Wcq, bcq, Wcv, bcv, Wp, bp):
        import jax, jax.numpy as jnp
        import numpy as np
        B, T, TC, C, CC, H = (2, 512, 128, 256, 128, 16)
        D = C // H

        def _heads(t):
            b, l, _ = t.shape
            return t.reshape(b, l, H, D).transpose(0, 2, 1, 3)
        scale = np.float32(1.0 / np.sqrt(D))
        q = _heads(x @ Wq + bq)
        k = _heads(x @ Wk + bk)
        v = _heads(x @ Wv + bv)
        att = jnp.einsum('bhqd,bhkd->bhqk', q, k) * scale
        causal = jnp.tril(jnp.ones((T, T), bool))
        att = jnp.where(causal[None, None], att, -jnp.inf)
        y = jnp.einsum('bhqk,bhkd->bhqd', jax.nn.softmax(att, axis=-1), v)
        qc = _heads(x @ Wcq + bcq)
        kc = _heads(cross_input @ Wck + bck)
        vc = _heads(cross_input @ Wcv + bcv)
        attc = jnp.einsum('bhqd,bhkd->bhqk', qc, kc) * scale
        y = y + jnp.einsum('bhqk,bhkd->bhqd', jax.nn.softmax(attc, axis=-1), vc)
        y = y.transpose(0, 2, 1, 3).reshape(x.shape[0], T, C)
        return y @ Wp + bp

    def _L0_ffn_ref(x, sg, su, sd, rg, ru, rd, wr, rb):
        import jax, jax.numpy as jnp
        import numpy as np
        H, I, E_ROUTED, TOP_K = (256, 704, 7, 2)
        B, S = (4, 512)

        def _expert(h, g, u, d):
            return jnp.einsum('...i,hi->...h', jax.nn.silu(h @ g.T) * (h @ u.T), d)
        shared_out = _expert(x, sg, su, sd)
        logits = x @ wr.T + rb
        probs = jax.nn.softmax(logits, axis=-1)
        scores, idx = jax.lax.top_k(probs, TOP_K)
        scores = scores / scores.sum(axis=-1, keepdims=True)
        w = jnp.sum(scores[..., None] * jax.nn.one_hot(idx, E_ROUTED, dtype=x.dtype), axis=-2)
        out = shared_out
        for e in range(E_ROUTED):
            out = out + w[..., e:e + 1] * _expert(x, rg[e], ru[e], rd[e])
        return out
    x = x + jnp.tanh(g_xattn[0]) * _L0_xattn_ref(_layernorm(x, axis=-1), ctx_512, L0_xattn_Wk, L0_xattn_bk, L0_xattn_Wq, L0_xattn_bq, L0_xattn_Wv, L0_xattn_bv, L0_xattn_Wck, L0_xattn_bck, L0_xattn_Wcq, L0_xattn_bcq, L0_xattn_Wcv, L0_xattn_bcv, L0_xattn_Wp, L0_xattn_bp)
    x = x + jnp.tanh(g_ffn[0]) * _L0_ffn_ref(_layernorm(x, axis=-1), L0_ffn_sg, L0_ffn_su, L0_ffn_sd, L0_ffn_rg, L0_ffn_ru, L0_ffn_rd, L0_ffn_wr, L0_ffn_rb)
    return x

_drawn_inputs = setup_inputs


def setup_inputs(seed=0):
    import zlib

    import numpy as np

    out = dict(_drawn_inputs(seed))
    spreads = {'L0_xattn_bk': (0.0, 2.0),
     'L0_xattn_bq': (0.0, 0.757),
     'L0_xattn_bv': (0.0, 0.1),
     'L0_xattn_bck': (0.0, 2.0),
     'L0_xattn_bcq': (0.0, 0.513),
     'L0_xattn_bcv': (0.0, 0.1),
     'L0_xattn_bp': (0.0, 0.1),
     'L0_ffn_rb': (0.0, 0.8)}
    factors = {'L0_ffn_rg': 3.334,
     'L0_ffn_ru': 3.29,
     'L0_ffn_rd': 3.293,
     'L0_ffn_wr': 4.006,
     'L0_ffn_sg': 2.79}
    for name, (base, spread) in spreads.items():
        noise = np.random.default_rng([zlib.crc32(name.encode()), seed]).standard_normal(out[name].shape)
        drawn = base * np.exp(spread * noise) if base else spread * noise
        out[name] = jnp.asarray(drawn.astype(out[name].dtype))
    for name, factor in factors.items():
        out[name] = (out[name] * factor).astype(out[name].dtype)
    return out
```

```python
from contextlib import ExitStack

import concourse.bass as bass
from concourse import mybir

F32 = mybir.dt.float32
BF16 = mybir.dt.bfloat16
ACT = mybir.ActivationFunctionType
ALU = mybir.AluOpType
AX_X = mybir.AxisListType.X

P = 128
B, T, C = 4, 512, 256
TC, CC = 1601, 128
H, D = 16, 16
NU = B * H
TT = T // P
NT = B * TT
CT = -(-TC // P)
CTAIL = TC - (CT - 1) * P
VT = TT + CT
NE, I = 8, 704
IT = -(-I // P)
ITAIL = I - (IT - 1) * P
SCALE = float(D) ** -0.5
EPS = 1e-5
LOW = -1e30
KROWS = 6 * D
MROWS = 2
VW = 32
NSEL = D + 1

CCH = [(0, 401), (401, 801), (801, 1201), (1201, 1601)]


def exp_groups():
    gs = [[(True, 2 * j, 0), (True, 2 * j + 1, 512)] for j in range(CT // 2)]
    gs.append([(True, CT - 1, 0)])
    gs.append([(False, 0, 0), (False, 1, 512)])
    gs.append([(False, 2, 0), (False, 3, 256)])
    return gs


GROUPS = exp_groups()
NG = len(GROUPS)
NMAX = TT * (len(CCH) + 1)
MAX_PER_GROUP = 3


def width(cross, kt):
    return T if cross else T - kt * P


def program(nc, a):
    ctx = ExitStack()
    with ctx:
        def sb(name, shape, dt=F32):
            return ctx.enter_context(nc.sbuf_tensor(name, shape, dt))

        def sem(name):
            return ctx.enter_context(nc.semaphore(name))

        q_parts = [nc.dram_tensor(f"q_parts{i}", (NU, 3 * D, T), BF16, kind="Internal").ap() for i in range(2)]
        k_parts = [nc.dram_tensor("k_parts0", (NU, 3 * D, T), BF16, kind="Internal").ap(),
                   nc.dram_tensor("k_parts1", (NU, 3 * D, TC), BF16, kind="Internal").ap()]

        ps = ctx.enter_context(nc.psum_tensor("ps", [P, 7, 512], F32))
        ps7 = ctx.enter_context(nc.psum_tensor("ps7", [P, 512], F32))

        x = sb("x", [P, NT, C])
        xnT = sb("xnT", [P, 2, B * T])
        shared = sb("shared", [P, NT * C])
        xn = shared[:, :].rearrange("p (t c) -> p t c", t=NT)
        y = shared[:, :].rearrange("p (u t d) -> p u t d", u=NU, t=TT)
        acc = xn
        arena = sb("arena", [P, NU * VT * D])
        v_all = arena[:, :].rearrange("p (u t d) -> p u t d", u=NU, t=VT)
        big = sb("big", [P, B * TC])
        ctxT = big
        ytok = big[:, 0:NT * C].rearrange("p (t c) -> p t c", t=NT)
        identb = sb("identb", [P, P], BF16)
        maskq = sb("maskq", [P, P], BF16)
        maskk = sb("maskk", [P, P], BF16)
        consts = sb("consts", [P, 3 * P])
        ident = consts[:, 0:P]
        sel = sb("sel", [P, 2 * NSEL])
        wq = sb("wq", [P, 3, 2, C])
        wck = sb("wck", [P, C])
        wv = sb("wv", [P, 2, C])
        wcv = sb("wcv", [P, C])
        wp = sb("wp", [P, 2, C])
        bqk = sb("bqk", [P, 4, 2])
        bv = sb("bv", [P, 3, C])
        gates = sb("gates", [P, 2])
        tg = sb("tg", [P, 2])
        wr = sb("wr", [P, 2, NE - 1])
        rb = sb("rb", [P, NE])
        desc = sb("desc", [P, NE])
        st = sb("st", [P, NT, 6])
        mv = sb("mv", [P, NT, 2])
        sd = sb("sd", [P, NT])
        rs = sb("rs", [P, NT])
        NB = 4
        work = sb("work", [P, 3 * 1024])
        hi, mid, lo = [work[:, 1024 * i:1024 * (i + 1)].bitcast(BF16).rearrange("p (b t) -> p b t", b=NB) for i in range(3)]
        res = sb("res", [P, NB, 512])
        qst = sb("qst", [P, 2, 2, T], BF16)
        kst = sb("kst", [P, 2, T], BF16)
        kcst = sb("kcst", [P, 2, TC], BF16)
        vst = sb("vst", [P, 2, VT, VW])
        pr = work[:, :].rearrange("p (b t) -> p b t", b=3)
        mx = sb("mx", [P, TT, len(CCH) + 1])
        mneg = sb("mneg", [P, 2, TT])
        mparts = sb("mparts", [P, 2, TT, MROWS], BF16)
        osb = sb("osb", [P, T])
        rsum = sb("rsum", [P, TT, 2])
        yc = sb("yc", [P, TT, D])
        ys = sb("ys", [P, TT, D])
        lg = sb("lg", [P, NT, NE])
        lg2 = sb("lg2", [P, NT, NE])
        key = sb("key", [P, NT, NE])
        s1 = sb("s1", [P, NT, NE])
        s2 = sb("s2", [P, NT, NE])
        wts = sb("wts", [P, NT, NE])
        m1 = sb("m1", [P, NT])
        m2 = sb("m2", [P, NT])
        km = sb("km", [P, NT])
        e2 = sb("e2", [P, NT])
        rd = sb("rd", [P, NT])
        sg = sb("sg", [P, 2, T])

        WUP = 2 * I
        WDN = IT * C
        def wview(par, off, n):
            o = par * (2 * WUP + WDN) + off
            return arena[:, o:o + n]
        wg_e = [wview(p, 0, WUP).rearrange("p (k i) -> p k i", k=2) for p in range(2)]
        wu_e = [wview(p, WUP, WUP).rearrange("p (k i) -> p k i", k=2) for p in range(2)]
        wd_e = [wview(p, 2 * WUP, WDN).rearrange("p (i c) -> p i c", i=IT) for p in range(2)]
        hT = [big[:, p * IT * T:(p + 1) * IT * T].rearrange("p (i t) -> p i t", i=IT) for p in range(2)]

        names = ("loaded x_loaded setup_done ln_done std_ready sqrt_done prep_mm prep_freed hi_done mid_done "
                 "split_done scr0 scr1 scr2 scr3 stack0 stack1 v_ready qk_done exp_done pv_done max_mm max_red "
                 "m_all m_hi m_split rows_tr rows_ready o_evac norm_mm rsum_ready y_parts y_done y_tokens dve_chain "
                 "pool_chain tail_mm tail_freed x2_ready tanh_done logits_mm gap_ready exp2_done "
                 "wload0 wload1 up_mm silu_done h_done down_mm acc_done stored").split()
        S = {n: sem(n) for n in names}
        scr = [S[f"scr{i}"] for i in range(NB)]
        stack = [S["stack0"], S["stack1"]]
        wload = [S["wload0"], S["wload1"]]
        block = ctx.enter_context(nc.Block())

        weight_loads = [
            (consts[:, :], a["consts"]), (sel[:, :], a["sel"]), (desc[:, :], a["desc"]),
            (wq[:, 0], a["Wq"].rearrange("(k p) c -> p k c", p=P)),
            (wq[:, 1], a["Wcq"].rearrange("(k p) c -> p k c", p=P)),
            (wq[:, 2], a["Wk"].rearrange("(k p) c -> p k c", p=P)),
            (wck[:, :], a["Wck"]), (wv[:, :, :], a["Wv"].rearrange("(k p) c -> p k c", p=P)),
            (wcv[:, :], a["Wcv"]), (wp[:, :, :], a["Wp"].rearrange("(k p) c -> p k c", p=P)),
            (bqk[:, :, :], a["bqk"]), (bv[:, :, :], a["bvp"]), (gates[:, :], a["gates"]),
            (wr[:, :, :], a["wrT"].rearrange("(k p) e -> p k e", p=P)), (rb[:, :], a["rb"]),
            (ctxT[:, :], a["ctxT"]),
        ]
        LOADED = 16 * len(weight_loads)

        pieces = []
        for b in range(B):
            pieces += [("turn", b, k) for k in range(2)]
            pieces += [("split", b, t, hf, 0, T) for t in range(3) for hf in range(2)]
            pieces += [("split", b, 3, hf, c0, c1) for hf in range(2) for c0, c1 in CCH]
            pieces += [("value", b, t) for t in range(VT)]
        split_of = {}
        for n, p in enumerate(pieces):
            if p[0] == "split":
                split_of[n] = len(split_of)
        NSPLIT = len(split_of)
        turn_end = {b: 1 + max(n for n, p in enumerate(pieces) if p[:2] == ("turn", b)) for b in range(B)}

        def scratch(b, t, hf, part, c0, c1):
            dst = (q_parts[0], q_parts[1], k_parts[0], k_parts[1])[t]
            row = part if t < 2 else 2 - part
            u0 = b * H + hf * (H // 2)
            return dst[u0:u0 + H // 2, row * D:(row + 1) * D, c0:c1]

        @block.sync
        def _(sp):
            sp.dma_start(x[:, :, :], a["x"].rearrange("(t p) c -> p t c", p=P)).then_inc(S["x_loaded"], 16)
            for dst, src in weight_loads:
                sp.dma_start(dst, src).then_inc(S["loaded"], 16)
            for n, p in enumerate(pieces):
                if p[0] != "split":
                    continue
                _, b, t, hf, c0, c1 = p
                s = split_of[n]
                sp.wait_ge(S["split_done"], s + 1)
                for part, buf in enumerate((hi, mid, lo)):
                    sp.dma_start(scratch(b, t, hf, part, c0, c1), buf[:, s % NB, 0:c1 - c0]).then_inc(scr[s % NB], 16)
            for i in range(NB):
                sp.wait_ge(scr[i], 48 * len(range(i, NSPLIT, NB)))

            def stack_loads(u, par):
                runs = [(0, 48, 0, 48), (48, 80, 0, 32), (80, 96, 0, 16)]
                for d0, d1, r0, r1 in runs:
                    for i in range(2):
                        sp.dma_start(qst[d0:d1, par, i, :],
                                     q_parts[i][bass.ds(u, 1), r0:r1, :].rearrange("a r t -> (a r) t")
                                     ).then_inc(stack[par], 16)
                    n = r1 - r0
                    sp.dma_start(kst[d0:d1, par, :],
                                 k_parts[0][bass.ds(u, 1), 48 - n:48, :].rearrange("a r t -> (a r) t")
                                 ).then_inc(stack[par], 16)
                    sp.dma_start(kcst[d0:d1, par, :],
                                 k_parts[1][bass.ds(u, 1), 48 - n:48, :].rearrange("a r t -> (a r) t")
                                 ).then_inc(stack[par], 16)

            stack_loads(0, 0)
            stack_loads(1, 1)
            with sp.Fori(0, NU // 2 - 1) as i:
                for par in range(2):
                    sp.wait_ge(S["qk_done"], i * (2 * NG) + NG * (par + 1))
                    stack_loads(i * 2 + (par + 2), par)

            def expert_loads(e, par):
                sp.dma_start(wg_e[par], a["eg"][bass.ds(e, 1)].rearrange("a (k p) i -> p (a k) i", p=P)).then_inc(wload[par], 16)
                sp.dma_start(wu_e[par], a["eu"][bass.ds(e, 1)].rearrange("a (k p) i -> p (a k) i", p=P)).then_inc(wload[par], 16)
                sp.dma_start(wd_e[par][:, 0:IT - 1, :],
                             a["ed"][bass.ds(e, 1), 0:(IT - 1) * P].rearrange("a (i p) c -> p (a i) c", p=P)).then_inc(wload[par], 16)
                sp.dma_start(wd_e[par][0:ITAIL, IT - 1, :],
                             a["ed"][bass.ds(e, 1), (IT - 1) * P:I].rearrange("a p c -> (a p) c")).then_inc(wload[par], 16)

            sp.wait_ge(S["pv_done"], NU * NG)
            expert_loads(0, 0)
            expert_loads(1, 1)
            with sp.Fori(0, NE // 2 - 1) as i:
                for par in range(2):
                    sp.wait_ge(S["down_mm"], i * 8 + 4 * (par + 1))
                    expert_loads(i * 2 + (par + 2), par)
            for t in range(NT):
                sp.wait_ge(S["x2_ready"], NT + t + 1)
                sp.dma_start(a["out"].rearrange("(t p) c -> p t c", p=P)[:, t, :], x[:, t, :]).then_inc(S["stored"], 16)
            sp.wait_ge(S["stored"], 16 * NT)

        @block.tensor
        def _(pe):
            def layer_turn(bank, b, k):
                for t in range(TT):
                    mm = pe.transpose(bank[:, t * P:(t + 1) * P], xn[:, b * TT + t, k * P:(k + 1) * P], ident)
                return mm

            pe.wait_ge(S["loaded"], LOADED)
            for n, p in enumerate(pieces):
                bk = ps[:, n % 7, :]
                if n >= 7:
                    pe.wait_ge(S["prep_freed"], n - 6)
                b = p[1]
                if p[0] == "turn":
                    if n == 0:
                        pe.wait_ge(S["ln_done"], NT)
                    mm = layer_turn(bk, b, p[2])
                elif p[0] == "split":
                    _, _, t, hf, c0, c1 = p
                    pe.wait_ge(S["prep_freed"], turn_end[b])
                    if t < 3:
                        for k in range(2):
                            mm = pe.matmul(bk, wq[:, t, k, hf * P:(hf + 1) * P], xnT[:, k, b * T:(b + 1) * T],
                                           start=(k == 0), stop=(k == 1))
                    else:
                        mm = pe.matmul(bk[:, 0:c1 - c0], wck[:, hf * P:(hf + 1) * P],
                                       ctxT[:, b * TC + c0:b * TC + c1], start=True, stop=True)
                else:
                    t = p[2]
                    if t < TT:
                        for k in range(2):
                            mm = pe.matmul(bk[:, 0:C], xnT[:, k, b * T + t * P:b * T + (t + 1) * P], wv[:, k, :],
                                           start=(k == 0), stop=(k == 1))
                    else:
                        k0 = (t - TT) * P
                        kn = min(P, TC - k0)
                        mm = pe.matmul(bk[0:kn, 0:C], ctxT[:, b * TC + k0:b * TC + k0 + kn], wcv[:, :],
                                       start=True, stop=True)
                mm.then_inc(S["prep_mm"], 1)

            def max_piece(v, vp, c):
                qt, j = divmod(c, len(CCH) + 1)
                out = ps[:, 4 + c % 2, :]
                pe.wait_ge(S["max_red"], v * NMAX + (c - 1))
                if j < len(CCH):
                    c0, c1 = CCH[j]
                    mm = pe.matmul(out[:, 0:c1 - c0], qst[0:KROWS, vp, 1, qt * P:(qt + 1) * P], kcst[0:KROWS, vp, c0:c1],
                                   start=True, stop=True)
                else:
                    n = (qt + 1) * P
                    pe.matmul(out[:, 0:n], qst[0:KROWS, vp, 0, qt * P:(qt + 1) * P], kst[0:KROWS, vp, 0:n],
                              start=True, stop=False)
                    mm = pe.matmul(out[:, n - P:n], identb[:, :], maskq[:, :], start=False, stop=True)
                mm.then_inc(S["max_mm"], 1)

            def scores(u, up, g):
                buf = (up + g) % 2
                for cross, kt, c0 in GROUPS[g]:
                    bk = ps[:, 2 * buf + c0 // 512, :]
                    o0 = c0 % 512
                    w = width(cross, kt)
                    if cross:
                        kn = min(P, TC - kt * P)
                        mm = pe.matmul(bk[0:kn, 0:w], kcst[0:KROWS + MROWS, up, kt * P:kt * P + kn],
                                       qst[0:KROWS + MROWS, up, 1, :], start=True, stop=True)
                    else:
                        pe.matmul(bk[:, o0:o0 + w], kst[0:KROWS + MROWS, up, kt * P:(kt + 1) * P],
                                  qst[0:KROWS + MROWS, up, 0, kt * P:T], start=True, stop=False)
                        mm = pe.matmul(bk[:, o0:o0 + P], identb[:, :], maskk[:, :], start=False, stop=True)
                mm.then_inc(S["qk_done"], 1)

            def values(up, g):
                for cross, kt, c0 in GROUPS[g]:
                    pb = pr[:, g % 3, c0:c0 + width(cross, kt)]
                    if cross:
                        q = kt % 3
                        kn = min(P, TC - kt * P)
                        mm = pe.matmul(ps[32 * q:32 * q + VW, 6, :], vst[0:kn, up, TT + kt, :], pb[0:kn, :],
                                       start=(kt < 3), stop=(kt >= CT - 3))
                    else:
                        mm = pe.matmul(ps[96:96 + VW, 6, kt * P:T], vst[:, up, kt, :], pb,
                                       start=(kt == 0), stop=(kt == TT - 1))
                mm.then_inc(S["pv_done"], 1)

            def max_rows(v):
                pe.wait_ge(S["m_split"], v + 1)
                for i in range(2):
                    for t in range(TT):
                        r = 64 + 32 * i
                        mm = pe.matmul(ps7[r:r + MROWS, t * P:(t + 1) * P], mparts[:, i, t, :], identb[:, :],
                                       start=True, stop=True)
                mm.then_inc(S["rows_tr"], 1)

            def step(u, up, prev, nxt):
                c = 0
                for g in range(NG):
                    if g == 0:
                        pe.wait_ge(S["rows_ready"], u * 2 + 2)
                    if prev or g >= 2:
                        pe.wait_ge(S["exp_done"], u * NG + (g - 1))
                    scores(u, up, g)
                    if nxt and g < NG - 2:
                        if g == 0:
                            pe.wait_ge(stack[1 - up], pair_value(u + 1, up))
                        for _ in range(MAX_PER_GROUP):
                            if c < NMAX:
                                max_piece(u + 1, 1 - up, c)
                                c += 1
                    if prev and g == 2:
                        pe.wait_ge(S["o_evac"], u)
                        norm(u)
                    if g == 1:
                        pe.wait_ge(S["v_ready"], u + 1)
                        if prev:
                            pe.wait_ge(S["o_evac"], u)
                    if g == NG - 1 and nxt:
                        if prev:
                            pe.wait_ge(S["y_parts"], u * 2)
                        max_rows(u + 1)
                    if g >= 1:
                        pe.wait_ge(S["exp_done"], u * NG + g)
                        values(up, g - 1)
                pe.wait_ge(S["exp_done"], u * NG + NG)
                values(up, NG - 1)

            def pair_value(v, up):
                return (v - (1 - up)) * 96 + 192

            def norm(u):
                for t in range(TT):
                    mm = pe.matmul(ps7[:, t * 2 * NSEL:(t + 1) * 2 * NSEL], osb[:, t * P:(t + 1) * P], sel[:, :],
                                   start=True, stop=True)
                mm.then_inc(S["norm_mm"], 1)

            pe.wait_ge(S["prep_freed"], len(pieces))
            pe.wait_ge(S["pool_chain"], 5)
            pe.wait_ge(S["setup_done"], 1)
            pe.wait_ge(stack[0], 192)
            for c in range(NMAX):
                if c < 2:
                    qt, j = divmod(c, len(CCH) + 1)
                    c0, c1 = CCH[j]
                    pe.matmul(ps[:, 4 + c, 0:c1 - c0], qst[0:KROWS, 0, 1, 0:P], kcst[0:KROWS, 0, c0:c1],
                              start=True, stop=True).then_inc(S["max_mm"], 1)
                else:
                    max_piece(0, 0, c)
            max_rows(0)
            step(0, 0, False, True)
            with pe.Fori(0, NU // 2 - 1) as i:
                step(i * 2 + 1, 1, True, True)
                step(i * 2 + 2, 0, True, True)
            step(NU - 1, 1, True, False)
            pe.wait_ge(S["o_evac"], NU)
            norm(NU)

            pe.wait_ge(S["y_tokens"], B)
            for n in range(8):
                b, k = divmod(n, 2)
                bk = ps[:, n % 4, :]
                if n >= 4:
                    pe.wait_ge(S["tail_freed"], n - 3)
                for t in range(TT):
                    mm = pe.transpose(bk[:, t * P:(t + 1) * P], ytok[:, b * TT + t, k * P:(k + 1) * P], ident)
                mm.then_inc(S["tail_mm"], 1)
            for t in range(NT):
                bk = ps[:, 4 + t % 2, 0:C]
                pe.wait_ge(S["tail_freed"], 8 if t < 2 else 8 + t - 1)
                for k in range(2):
                    mm = pe.matmul(bk, xnT[:, k, t * P:(t + 1) * P], wp[:, k, :], start=(k == 0), stop=(k == 1))
                mm.then_inc(S["tail_mm"], 1)
            pe.wait_ge(S["ln_done"], 2 * NT)
            for n in range(8):
                b, k = divmod(n, 2)
                if n >= 4:
                    pe.wait_ge(S["tail_freed"], 8 + NT + n - 3)
                layer_turn(ps[:, n % 4, :], b, k).then_inc(S["tail_mm"], 1)
            pe.wait_ge(S["tail_freed"], 16 + NT)
            for t in range(NT):
                for k in range(2):
                    mm = pe.matmul(ps7[:, t * NE:t * NE + NE - 1], xnT[:, k, t * P:(t + 1) * P], wr[:, k, :],
                                   start=(k == 0), stop=(k == 1))
            mm.then_inc(S["logits_mm"], 1)

            def expert(e, par, first):
                pe.wait_ge(wload[par], (e - par) * 32 + 64)
                for tb in range(B):
                    for it in range(IT):
                        m = min(P, I - it * P)
                        k0 = tb * IT + it
                        if not (first and k0 < 2):
                            pe.wait_ge(S["h_done"], e * (B * IT) + (k0 - 1))
                        for j, w in enumerate((wg_e[par], wu_e[par])):
                            for k in range(2):
                                mm = pe.matmul(ps[0:m, 2 * (k0 % 2) + j, :], w[:, k, it * P:it * P + m],
                                               xnT[:, k, tb * T:(tb + 1) * T], start=(k == 0), stop=(k == 1))
                        mm.then_inc(S["up_mm"], 1)
                    if not (first and tb == 0):
                        pe.wait_ge(S["acc_done"], e * B + tb)
                    pe.wait_ge(S["h_done"], e * (B * IT) + (tb + 1) * IT)
                    for t in range(TT):
                        out = ps[:, 4 + t // 2, (t % 2) * C:(t % 2 + 1) * C]
                        for it in range(IT):
                            m = min(P, I - it * P)
                            mm = pe.matmul(out, hT[tb % 2][0:m, it, t * P:(t + 1) * P], wd_e[par][0:m, it, :],
                                           start=(it == 0), stop=(it == IT - 1))
                    mm.then_inc(S["down_mm"], 1)

            expert(0, 0, True)
            expert(1, 1, False)
            with pe.Fori(1, NE // 2) as i:
                expert(i * 2, 0, False)
                expert(i * 2 + 1, 1, False)

        @block.scalar
        def _(act):
            act.wait_ge(S["std_ready"], 1)
            act.activation(sd[:, :], sd[:, :], ACT.Sqrt).then_inc(S["sqrt_done"], 1)
            for n, p in enumerate(pieces):
                if p[0] != "split":
                    continue
                _, b, t, hf, c0, c1 = p
                s = split_of[n]
                act.wait_ge(S["prep_mm"], n + 1)
                if s >= NB:
                    act.wait_ge(scr[s % NB], 48 * (s // NB))
                act.activation(hi[:, s % NB, 0:c1 - c0], ps[:, n % 7, 0:c1 - c0], ACT.Identity,
                               bias=bqk[:, t, hf:hf + 1]).then_inc(S["hi_done"], 1)

            def rows(v, vp):
                act.wait_ge(S["rows_tr"], v + 1)
                for i in range(2):
                    r = 64 + 32 * i
                    act.activation(qst[KROWS:KROWS + MROWS, vp, i, :], ps7[r:r + MROWS, :], ACT.Copy
                                   ).then_inc(S["rows_ready"], 1)

            def step(u, up, prev, nxt):
                for g in range(NG):
                    buf = (up + g) % 2
                    act.wait_ge(S["qk_done"], u * NG + (g + 1))
                    if prev or g >= 3:
                        act.wait_ge(S["pv_done"], u * NG + (g - 2))
                    cross, kt, c0 = GROUPS[g][-1]
                    n = c0 + width(cross, kt)
                    kn = CTAIL if cross and kt == CT - 1 else P
                    act.activation(pr[0:kn, g % 3, 0:n],
                                   ps[0:kn, 2 * buf:2 * buf + 2, :].rearrange("p b n -> p (b n)")[:, 0:n],
                                   ACT.Exp, scale=SCALE).then_inc(S["exp_done"], 1)
                if nxt:
                    rows(u + 1, 1 - up)

            rows(0, 0)
            step(0, 0, False, True)
            with act.Fori(0, NU // 2 - 1) as i:
                step(i * 2 + 1, 1, True, True)
                step(i * 2 + 2, 0, True, True)
            step(NU - 1, 1, True, False)
            act.activation(tg[:, :], gates[:, :], ACT.Tanh).then_inc(S["tanh_done"], 1)
            act.wait_ge(S["std_ready"], 2)
            act.activation(sd[:, :], sd[:, :], ACT.Sqrt).then_inc(S["sqrt_done"], 1)
            act.wait_ge(S["gap_ready"], 1)
            act.activation(e2[:, :], e2[:, :], ACT.Exp).then_inc(S["exp2_done"], 1)

            def expert(e, first):
                for k0 in range(B * IT):
                    m = ITAIL if k0 % IT == IT - 1 else P
                    act.wait_ge(S["up_mm"], e * (B * IT) + (k0 + 1))
                    if not (first and k0 < 2):
                        act.wait_ge(S["h_done"], e * (B * IT) + (k0 - 1))
                    act.activation(sg[0:m, k0 % 2, :], ps[0:m, 2 * (k0 % 2), :], ACT.Silu).then_inc(S["silu_done"], 1)

            expert(0, True)
            with act.Fori(1, NE) as e:
                expert(e, False)

        @block.gpsimd
        def _(pool):
            pool.memset(v_all[:, :, VT - 1, :], 0.0).then_inc(S["pool_chain"], 1)
            pool.wait_ge(S["pool_chain"], 1)
            pool.memset(vst[:, :, :, D + 1:VW], 0.0).then_inc(S["pool_chain"], 1)
            pool.wait_ge(S["pool_chain"], 2)
            pool.memset(vst[:, :, :, D:D + 1], 1.0).then_inc(S["pool_chain"], 1)
            pool.wait_ge(S["pool_chain"], 3)
            pool.memset(kst[KROWS:KROWS + MROWS, :, :], 1.0).then_inc(S["pool_chain"], 1)
            pool.wait_ge(S["pool_chain"], 4)
            pool.memset(kcst[KROWS:KROWS + MROWS, :, :], 1.0).then_inc(S["pool_chain"], 1)
            pool.wait_ge(S["pool_chain"], 5)
            for n, p in enumerate(pieces):
                if p[0] != "split":
                    continue
                _, b, t, hf, c0, c1 = p
                s = split_of[n]
                w = c1 - c0
                pool.wait_ge(S["prep_freed"], n + 1)
                if s >= NB:
                    pool.wait_ge(scr[s % NB], 48 * (s // NB))
                if s:
                    pool.wait_ge(S["split_done"], s)
                pool.tensor_copy(mid[:, s % NB, 0:w], res[:, s % NB, 0:w]).then_inc(S["mid_done"], 1)
                pool.wait_ge(S["mid_done"], s + 1)
                pool.tensor_tensor(lo[:, s % NB, 0:w], res[:, s % NB, 0:w], mid[:, s % NB, 0:w],
                                   ALU.subtract).then_inc(S["split_done"], 1)

        @block.vector
        def _(dve):
            chain = [0]

            def link(ins):
                chain[0] += 1
                ins.then_inc(S["dve_chain"], 1)
                dve.wait_ge(S["dve_chain"], chain[0])

            def layernorm(k):
                for t in range(NT):
                    link(dve.bn_stats(st[:, t, :], x[:, t, :]))
                    link(dve.bn_aggr(mv[:, t, :], st[:, t, :]))
                dve.tensor_scalar(sd[:, :], mv[:, :, 1], EPS, None, ALU.add).then_inc(S["std_ready"], 1)
                dve.wait_ge(S["sqrt_done"], k)
                link(dve.reciprocal(rs[:, :], sd[:, :]))
                for t in range(NT):
                    dve.tensor_scalar(xn[:, t, :], x[:, t, :], mv[:, t, 0:1], rs[:, t:t + 1],
                                      ALU.subtract, ALU.mult).then_inc(S["ln_done"], 1)

            dve.wait_ge(S["x_loaded"], 16)
            layernorm(1)
            dve.wait_ge(S["loaded"], LOADED)
            dve.tensor_copy(maskq[:, :], consts[:, P:2 * P])
            dve.tensor_copy(maskk[:, :], consts[:, 2 * P:3 * P])
            dve.tensor_copy(identb[:, :], consts[:, 0:P]).then_inc(S["setup_done"], 1)
            dve.wait_ge(S["pool_chain"], 1)
            for n, p in enumerate(pieces):
                bk = ps[:, n % 7, :]
                b = p[1]
                dve.wait_ge(S["prep_mm"], n + 1)
                if p[0] == "turn":
                    dve.tensor_copy(xnT[:, p[2], b * T:(b + 1) * T], bk).then_inc(S["prep_freed"], 1)
                elif p[0] == "split":
                    _, _, t, hf, c0, c1 = p
                    s = split_of[n]
                    dve.wait_ge(S["hi_done"], s + 1)
                    if s >= NB:
                        dve.wait_ge(S["split_done"], s - NB + 1)
                    dve.scalar_tensor_tensor(out=res[:, s % NB, 0:c1 - c0], in0=bk[:, 0:c1 - c0],
                                             scalar=bqk[:, t, hf:hf + 1], in1=hi[:, s % NB, 0:c1 - c0],
                                             op0=ALU.add, op1=ALU.subtract).then_inc(S["prep_freed"], 1)
                else:
                    t = p[2]
                    kn = CTAIL if t == VT - 1 else P
                    dve.tensor_tensor(v_all[0:kn, b * H:(b + 1) * H, t, :],
                                      bk[0:kn, 0:C].rearrange("p (h d) -> p h d", h=H),
                                      bv[0:kn, 0 if t < TT else 1, :].rearrange("p (h d) -> p h d", h=H),
                                      ALU.add).then_inc(S["prep_freed"], 1)

            def value_copy(v, vp):
                dve.tensor_copy(vst[:, vp:vp + 1, :, 0:D], v_all[:, bass.ds(v, 1), :, :]).then_inc(S["v_ready"], 1)

            def reduce_piece(v, c):
                qt, j = divmod(c, len(CCH) + 1)
                dve.wait_ge(S["max_mm"], v * NMAX + (c + 1))
                if j < len(CCH):
                    out, w = mx[:, qt, j:j + 1], CCH[j][1] - CCH[j][0]
                else:
                    out, w = mneg[:, 0, qt:qt + 1], (qt + 1) * P
                dve.tensor_reduce(out, ps[:, 4 + c % 2, 0:w], AX_X, ALU.max).then_inc(S["max_red"], 1)

            def max_parts(v):
                dve.wait_ge(S["max_red"], v * NMAX + NMAX)
                dve.tensor_reduce(mneg[:, 1, :], mx[:, :, 0:len(CCH)], AX_X, ALU.max).then_inc(S["m_all"], 1)
                dve.wait_ge(S["m_all"], v + 1)
                dve.tensor_scalar(mparts[:, :, :, 0], mneg[:, :, :], -1.0, None, ALU.mult).then_inc(S["m_hi"], 1)
                dve.wait_ge(S["m_hi"], v + 1)
                dve.scalar_tensor_tensor(out=mparts[:, :, :, 1], in0=mneg[:, :, :], scalar=-1.0, in1=mparts[:, :, :, 0],
                                         op0=ALU.mult, op1=ALU.subtract).then_inc(S["m_split"], 1)

            def sums_out(u):
                dve.wait_ge(S["pv_done"], u * NG)
                dve.tensor_copy(osb[:, :], ps[:, 6, :]).then_inc(S["o_evac"], 1)

            def outputs(u):
                nm = ps7[:, 0:TT * 2 * NSEL].rearrange("p (t s d) -> p t s d", t=TT, s=2)
                dve.wait_ge(S["norm_mm"], u)
                dve.reciprocal(rsum[:, :, :], nm[:, :, :, D]).then_inc(S["rsum_ready"], 1)
                dve.wait_ge(S["rsum_ready"], u)
                for i, part in enumerate((yc, ys)):
                    dve.tensor_tensor(part[:, :, :], nm[:, :, i, 0:D],
                                      rsum[:, :, i:i + 1].to_broadcast([P, TT, D]), ALU.mult).then_inc(S["y_parts"], 1)
                dve.wait_ge(S["y_parts"], u * 2)
                dve.tensor_tensor(y[:, bass.ds(u - 1, 1), :, :], yc[:, :, :], ys[:, :, :], ALU.add).then_inc(S["y_done"], 1)

            def step(u, up, prev, nxt):
                if prev:
                    sums_out(u)
                if nxt:
                    value_copy(u + 1, 1 - up)
                for c in range(NMAX if nxt else 0):
                    reduce_piece(u + 1, c)
                    if prev and c == 3 * MAX_PER_GROUP - 1:
                        outputs(u)
                if prev and not nxt:
                    outputs(u)
                if nxt:
                    max_parts(u + 1)

            dve.wait_ge(S["prep_freed"], len(pieces))
            value_copy(0, 0)
            for c in range(NMAX):
                reduce_piece(0, c)
            max_parts(0)
            step(0, 0, False, True)
            with dve.Fori(0, NU // 2 - 1) as i:
                step(i * 2 + 1, 1, True, True)
                step(i * 2 + 2, 0, True, True)
            step(NU - 1, 1, True, False)
            sums_out(NU)
            outputs(NU)

            dve.wait_ge(S["tanh_done"], 1)
            dve.wait_ge(S["y_done"], NU)
            for b in range(B):
                dve.tensor_copy(ytok[:, b * TT:(b + 1) * TT, :].rearrange("p t (h d) -> p t h d", h=H),
                                y[:, b * H:(b + 1) * H, :, :].rearrange("p h t d -> p t h d")).then_inc(S["y_tokens"], 1)
            for n in range(8):
                b, k = divmod(n, 2)
                dve.wait_ge(S["tail_mm"], n + 1)
                dve.tensor_copy(xnT[:, k, b * T:(b + 1) * T], ps[:, n % 4, :]).then_inc(S["tail_freed"], 1)
            for t in range(NT):
                dve.wait_ge(S["tail_mm"], 9 + t)
                row = osb[:, (t % 2) * C:(t % 2 + 1) * C]
                if t >= 2:
                    dve.wait_ge(S["x2_ready"], t - 1)
                dve.tensor_tensor(row, ps[:, 4 + t % 2, 0:C], bv[:, 2, :], ALU.add).then_inc(S["tail_freed"], 1)
                dve.wait_ge(S["tail_freed"], 9 + t)
                dve.scalar_tensor_tensor(out=x[:, t, :], in0=row, scalar=tg[:, 0:1], in1=x[:, t, :],
                                         op0=ALU.mult, op1=ALU.add).then_inc(S["x2_ready"], 1)
            dve.wait_ge(S["x2_ready"], NT)
            layernorm(2)
            for n in range(8):
                b, k = divmod(n, 2)
                dve.wait_ge(S["tail_mm"], 9 + NT + n)
                dve.tensor_copy(xnT[:, k, b * T:(b + 1) * T], ps[:, n % 4, :]).then_inc(S["tail_freed"], 1)
            link(dve.memset(lg[:, :, NE - 1:NE], -3e38))
            dve.wait_ge(S["logits_mm"], 1)
            link(dve.tensor_tensor(lg[:, :, 0:NE - 1], ps7[:, 0:NT * NE].rearrange("p (t e) -> p t e", t=NT)[:, :, 0:NE - 1],
                                   rb[:, 0:NE - 1].unsqueeze(1).to_broadcast([P, NT, NE - 1]), ALU.add))

            def first_largest(src, m, s):
                full = [P, NT, NE]
                link(dve.tensor_reduce(m[:, :], src[:, :, :], AX_X, ALU.max))
                link(dve.tensor_tensor(s[:, :, :], src[:, :, :], m[:, :].unsqueeze(2).to_broadcast(full), ALU.is_equal))
                link(dve.tensor_tensor(key[:, :, :], s[:, :, :], desc[:, :].unsqueeze(1).to_broadcast(full), ALU.mult))
                link(dve.tensor_reduce(km[:, :], key[:, :, :], AX_X, ALU.max))
                link(dve.tensor_tensor(s[:, :, :], key[:, :, :], km[:, :].unsqueeze(2).to_broadcast(full), ALU.is_equal))

            first_largest(lg, m1, s1)
            link(dve.scalar_tensor_tensor(out=lg2[:, :, :], in0=s1[:, :, :], scalar=-3e38, in1=lg[:, :, :],
                                          op0=ALU.mult, op1=ALU.add))
            first_largest(lg2, m2, s2)
            dve.tensor_tensor(e2[:, :], m2[:, :], m1[:, :], ALU.subtract).then_inc(S["gap_ready"], 1)
            dve.wait_ge(S["exp2_done"], 1)
            link(dve.tensor_scalar(rd[:, :], e2[:, :], 1.0, None, ALU.add))
            link(dve.reciprocal(rd[:, :], rd[:, :]))
            link(dve.tensor_tensor(e2[:, :], e2[:, :], rd[:, :], ALU.mult))
            link(dve.tensor_tensor(s1[:, :, :], s1[:, :, :], rd[:, :].unsqueeze(2).to_broadcast([P, NT, NE]), ALU.mult))
            link(dve.tensor_tensor(s2[:, :, :], s2[:, :, :], e2[:, :].unsqueeze(2).to_broadcast([P, NT, NE]), ALU.mult))
            link(dve.tensor_tensor(wts[:, :, 1:NE], s1[:, :, 0:NE - 1], s2[:, :, 0:NE - 1], ALU.add))
            link(dve.memset(wts[:, :, 0:1], 1.0))
            dve.wait_ge(S["tail_mm"], 16 + NT)
            link(dve.memset(shared[:, :], 0.0))

            def expert(e, first):
                for tb in range(B):
                    for it in range(IT):
                        k0 = tb * IT + it
                        m = min(P, I - it * P)
                        dve.wait_ge(S["silu_done"], e * (B * IT) + (k0 + 1))
                        if it == 0 and not (first and tb < 2):
                            dve.wait_ge(S["down_mm"], e * B + (tb - 1))
                        dve.tensor_tensor(hT[tb % 2][0:m, it, :], sg[0:m, k0 % 2, :], ps[0:m, 2 * (k0 % 2) + 1, :],
                                          ALU.mult).then_inc(S["h_done"], 1)
                    dve.wait_ge(S["down_mm"], e * B + (tb + 1))
                    for t in range(TT):
                        n = tb * TT + t
                        ins = dve.scalar_tensor_tensor(out=acc[:, n, :], in0=ps[:, 4 + t // 2, (t % 2) * C:(t % 2 + 1) * C],
                                                       scalar=wts[:, n, bass.ds(e, 1)], in1=acc[:, n, :],
                                                       op0=ALU.mult, op1=ALU.add)
                    ins.then_inc(S["acc_done"], 1)

            expert(0, True)
            with dve.Fori(1, NE) as e:
                expert(e, False)
            dve.wait_ge(S["acc_done"], NE * B)
            for t in range(NT):
                dve.scalar_tensor_tensor(out=x[:, t, :], in0=acc[:, t, :], scalar=tg[:, 1:2], in1=x[:, t, :],
                                         op0=ALU.mult, op1=ALU.add).then_inc(S["x2_ready"], 1)


def kernel(**inputs):
    import numpy as np
    import concourse.bacc as bacc
    from concourse.bass_utils import run_bass_kernel_spmd

    i = {k.replace("L0_xattn_", "").replace("L0_ffn_", ""): np.asarray(v) for k, v in inputs.items()}

    def over(v, n):
        return np.broadcast_to(v.reshape(1, n), (P, n))

    future = np.triu(np.full((P, P), LOW, np.float32), 1)
    consts = np.concatenate([np.eye(P, dtype=np.float32), future, future.T], axis=1)
    sel = np.zeros((P, 2 * NSEL), np.float32)
    for q in range(4):
        for d in range(NSEL):
            sel[32 * q + d, (q == 3) * NSEL + d] = 1.0
    arrays = {
        "x": i["x"].reshape(B * T, C),
        "ctxT": i["ctx_512"].transpose(2, 0, 1).reshape(CC, B * TC),
        "Wq": i["Wq"], "Wcq": i["Wcq"], "Wk": i["Wk"], "Wck": i["Wck"], "Wv": i["Wv"], "Wcv": i["Wcv"], "Wp": i["Wp"],
        "bqk": np.stack([i[n].reshape(2, P).T for n in ("bq", "bcq", "bk", "bck")], axis=1),
        "bvp": np.stack([over(i[n], C) for n in ("bv", "bcv", "bp")], axis=1),
        "gates": np.concatenate([over(i["g_xattn"], 1), over(i["g_ffn"], 1)], axis=1),
        "wrT": i["wr"].T,
        "rb": np.concatenate([over(i["rb"], NE - 1), np.zeros((P, 1), np.float32)], axis=1),
        "eg": np.concatenate([i["sg"][None], i["rg"]]).transpose(0, 2, 1),
        "eu": np.concatenate([i["su"][None], i["ru"]]).transpose(0, 2, 1),
        "ed": np.concatenate([i["sd"][None], i["rd"]]).transpose(0, 2, 1),
        "consts": consts, "sel": sel,
        "desc": over(np.arange(NE, 0, -1).astype(np.float32), NE),
    }
    arrays = {k: np.ascontiguousarray(v) for k, v in arrays.items()}
    nc = bacc.Bacc("TRN2", target_bir_lowering=False, num_devices=1)
    aps = {k: nc.dram_tensor("in_" + k, v.shape, F32, kind="ExternalInput").ap() for k, v in arrays.items()}
    aps["out"] = nc.dram_tensor("out", (B * T, C), F32, kind="ExternalOutput").ap()
    program(nc, aps)
    r = run_bass_kernel_spmd(nc, [{"in_" + k: v for k, v in arrays.items()}], core_ids=[0])
    return r.results[0]["out"].reshape(B, T, C)
```

```python
from contextlib import ExitStack

import numpy as np
import concourse.bass as bass
from concourse import mybir

F32 = mybir.dt.float32
BF16 = mybir.dt.bfloat16
U32 = mybir.dt.uint32
ACT = mybir.ActivationFunctionType
ALU = mybir.AluOpType
AX_X = mybir.AxisListType.X

P = 128
B, T, C = 4, 512, 256
TC, CC = 1601, 128
H, D = 16, 16
NB = 4
NU = B * H
TT = T // P
NT = B * TT
CT = -(-TC // P)
CTAIL = TC - (CT - 1) * P
VT = TT + CT
NE, I = 7, 704
TOP = 2
E8 = NE + 1
CH = I // 2
CUTS = [(c * CH + i, min(P, CH - i)) for c in range(2) for i in range(0, CH, P)]
IT = len(CUTS)
WE = 4 * I + IT * C
NTOK = B * T
NSLOT = (NTOK * TOP + NE * (P - 1)) // P
SHARED = NE
ROUTE_WIDTHS = [P, P, P, NT, E8 * E8, NSLOT, NSLOT + 1, TOP * NT, 1]
ROUTE_COLS = sum(ROUTE_WIDTHS)
ROUTE_AT = [(sum(ROUTE_WIDTHS[:i]), sum(ROUTE_WIDTHS[:i + 1])) for i in range(len(ROUTE_WIDTHS))]
SCALE = float(D) ** -0.5
EPS = 1e-5
LOW = -1e30
KROWS = 6 * D
MROWS = 2
VW = 32
NSEL = D + 1

CHUNK = 512
NCH = TC // CHUNK
TAIL = TC - NCH * CHUNK
MAX_PIECES = [("cross", qt, j) for qt in range(TT) for j in range(NCH)] + [("tail",), ("pair",), ("self", 2), ("self", 3)]
NMAX = len(MAX_PIECES)

X, Y = True, False
GROUPS = [[(X, 0, 0), (X, 1, 512)], [(X, 2, 0), (Y, 0, 512)], [(Y, 1, 0), (Y, 3, 384), (Y, 2, 512)],
          [(X, 3, 0), (X, 4, 512)], [(X, 5, 0), (X, 6, 512)], [(X, 7, 0), (X, 8, 512)],
          [(X, 9, 0), (X, 10, 512)], [(X, 11, 0), (X, 12, 512)]]
BUFFER = [0, 1, 2, 3, 4, 1, 5, 3]
BUF_AT = [0, 1024, 2048, 2816, 3840, 4864]
BUF_END = 5888
NG = len(GROUPS)
BATCHES = [[(X, 0), (X, 1), (X, 2), (Y, 0)], [(X, 3), (X, 4), (X, 5), (Y, 1)],
           [(X, 6), (X, 7), (X, 8), (Y, 2), (Y, 3)], [(X, 9), (X, 10), (X, 11), (X, 12)]]
AFTER = [1, 4, 5, 7]
NPV = 2 * len(BATCHES)
FREED = [-6, -2, -2, 0, -2, 2, 0, 4]
WHERE = {(c, kt): BUF_AT[BUFFER[g]] + c0 for g, grp in enumerate(GROUPS) for c, kt, c0 in grp}
NR = 3
CPAD = CT * P


HALF = NMAX // 2


def schedule():
    out = []
    for g in range(NG):
        tiles = [("score", g, i) for i in range(len(GROUPS[g]))]
        out += tiles[:1] + [("max", 2 * g)] + tiles[1:] + [("values", g - 3)]
        if g == 4:
            out.append(("norm",))
        if g == 6:
            out.append(("rows",))
        out.append(("max", 2 * g + 1))
    return out


OUTPUTS_AT = 9


def run_steps(eng, step):
    step(0, 0, False, True, True)
    with eng.Fori(0, NU // NR - 1) as i:
        for r in range(NR):
            step(i * NR + (r + 1), (r + 1) % NR, True, True, True)
    for u in range(NR * (NU // NR - 1) + 1, NU):
        step(u, u % NR, True, u + 1 < NU, u + 2 < NU)


PREP_CHUNKS = [(0, 401), (401, 801), (801, 1201), (1201, 1601)]


def width(cross, kt):
    return T if cross else T - kt * P


PE_ORDER = schedule()


def program(nc, a):
    ctx = ExitStack()
    with ctx:
        def sb(name, shape, dt=F32):
            return ctx.enter_context(nc.sbuf_tensor(name, shape, dt))

        def sem(name):
            return ctx.enter_context(nc.semaphore(name))

        q_parts = nc.dram_tensor("q_parts", (NU, 3 * D, 2 * T), BF16, kind="Internal").ap()
        k_parts = nc.dram_tensor("k_parts", (NU, 3 * D, T + TC), BF16, kind="Internal").ap()

        xn_rows = nc.dram_tensor("xn_rows", (NTOK, C), F32, kind="Internal").ap()
        y_rows = nc.dram_tensor("y_rows", (TOP * NTOK + P, C), F32, kind="Internal").ap()

        ps = ctx.enter_context(nc.psum_tensor("ps", [P, 7, 512], F32))
        ps7 = ctx.enter_context(nc.psum_tensor("ps7", [P, 512], F32))

        x = sb("x", [P, NT, C])
        xnT = sb("xnT", [P, 2, B * T])
        shared = sb("shared", [P, NT * C])
        xn = shared[:, :].rearrange("p (t c) -> p t c", t=NT)
        y = shared[:, :].rearrange("p (u t d) -> p u t d", u=NU, t=TT)
        acc = xn
        parts = [("values", NU * VT * D), ("big", B * TC), ("kst", NR * (T + CPAD) // 2), ("qst", NR * T),
                 ("vst", NR * VT * VW), ("wq", 6 * C), ("wck", C), ("wv", 2 * C), ("wcv", C), ("res", NB * 512)]
        place, end = {}, 0
        for part, n in parts:
            place[part] = (end, end + n)
            end += n
        arena = sb("arena", [P, max(end, (NE + 1) * WE)])

        def region(part):
            return arena[:, place[part][0]:place[part][1]]

        v_all = region("values").rearrange("p (u t d) -> p u t d", u=NU, t=VT)
        big = region("big")
        ctxT = big
        ytok = big[:, 0:NT * C].rearrange("p (t c) -> p t c", t=NT)
        identb = sb("identb", [P, P], BF16)
        maskq = sb("maskq", [P, 3 * P], BF16)
        maskk = sb("maskk", [P, P], BF16)
        ident = sb("ident", [P, P])
        masks = region("qst")[:, 0:4 * P]
        sel = sb("sel", [P, 2 * NSEL])
        wq = region("wq").rearrange("p (w k c) -> p w k c", w=3, k=2)
        wck = region("wck")
        wv = region("wv").rearrange("p (k c) -> p k c", k=2)
        wcv = region("wcv")
        wp = sb("wp", [P, 2, C])
        bqk = sb("bqk", [P, 4, 2])
        bv = sb("bv", [P, 3, C])
        gates = sb("gates", [P, 2])
        tg = sb("tg", [P, 2])
        wr = sb("wr", [P, 2, NE])
        rb = sb("rb", [P, E8])
        desc = sb("desc", [P, E8])
        st = sb("st", [P, NT, 6])
        mv = sb("mv", [P, NT, 2])
        sd = sb("sd", [P, NT])
        rs = sb("rs", [P, NT])
        work = sb("work", [P, 3 * 1024])
        hi, mid, lo = [work[:, 1024 * i:1024 * (i + 1)].bitcast(BF16).rearrange("p (b t) -> p b t", b=NB) for i in range(3)]
        res = region("res").rearrange("p (b t) -> p b t", b=NB)
        qst = region("qst").bitcast(BF16).rearrange("p (r i t) -> p r i t", r=NR, i=2)
        kst = region("kst").bitcast(BF16).rearrange("p (r t) -> p r t", r=NR)
        vst = region("vst").rearrange("p (r t w) -> p r t w", r=NR, t=VT)
        pr = big[:, 0:BUF_END]
        mx = sb("mx", [P, TT, NCH + 1])
        mneg = sb("mneg", [P, 2, TT])
        mparts = sb("mparts", [P, 2, TT, MROWS], BF16)
        osb = work[:, 2 * T:3 * T]
        rsum = sb("rsum", [P, TT, 2])
        yb = sb("yb", [P, 1, TT, 2, D])
        router = sb("router", [P, 4 * NT * E8])
        lg, key, s1, s2 = [router[:, NT * E8 * i:NT * E8 * (i + 1)].rearrange("p (t e) -> p t e", t=NT)
                        for i in range(4)]
        took = key
        m1 = sb("m1", [P, NT])
        m2 = sb("m2", [P, NT])
        km = sb("km", [P, NT])
        e2 = sb("e2", [P, NT])
        rd = sb("rd", [P, NT])
        weight = sb("weight", [P, TOP, NT])
        tile_expert = sb("tile_expert", [P, NSLOT], U32)
        slot_table = sb("slot_table", [P, NSLOT, 2], U32)
        rt_end = [(NE - 1) * WE]

        def rt(*shape):
            n = int(np.prod(shape))
            o = rt_end[0]
            rt_end[0] += n
            assert rt_end[0] <= NE * WE
            v = arena[:, o:o + n]
            if len(shape) == 2:
                v = v.rearrange("p (a b) -> p a b", a=shape[0])
            if len(shape) == 3:
                v = v.rearrange("p (a b c) -> p a b c", a=shape[0], b=shape[1])
            return v

        rconst = rt(ROUTE_COLS)
        before, ones, slot_of, bounds, below, tile_no, tile_begin, result_row, spare_row = [
            rconst[:, c0:c1] for c0, c1 in ROUTE_AT]
        counts = rt(NT + 1, E8)
        passed = rt(E8, NT)
        ntiles = rt(E8)
        earlier = rt(E8, E8)
        start = rt(E8)
        reached = rt(NSLOT, NE - 1)
        expert_no = rt(NSLOT)
        at = rt(NT, E8)
        taken = rt(NT, E8)
        slot = rt(TOP, NT)
        slot_tile = rt(TOP, NT)
        lane = rt(TOP, NT)
        from_tile = rt(NT, NSLOT + 1)
        row_in = rt(NT, NSLOT)
        in_lane = rt(2, 4, P)
        table = rt(NSLOT)
        empty = rt(NSLOT)
        result_at = rt(NSLOT)
        back = rt(NSLOT)

        weights = arena[:, 0:(NE + 1) * WE].rearrange("p (e w) -> p e w", e=NE + 1)
        wgs, wus = [weights[:, SHARED, 2 * I * j:2 * I * (j + 1)].rearrange("p (k i) -> p k i", k=2) for j in range(2)]
        wds = weights[:, SHARED, 4 * I:WE].rearrange("p (i c) -> p i c", i=IT)
        sg = shared[:, 0:2 * T].rearrange("p (b t) -> p b t", b=2)
        hT = [work[:, :].rearrange("p (i t) -> p i t", i=IT),
              shared[:, 2 * T:2 * T + IT * T].rearrange("p (i t) -> p i t", i=IT)]
        xg = wp
        yt = bv
        xgT = work[:, 0:4 * P].rearrange("p (b k t) -> p b k t", b=2, k=2)
        gate_s = work[:, 4 * P:4 * P + I].rearrange("p (c i) -> p c i", c=2)
        hid = work[:, 4 * P + I:4 * P + 2 * I].rearrange("p (c i) -> p c i", c=2)
        hidT = work[:, 4 * P + 2 * I:4 * P + 2 * I + IT * P].rearrange("p (i t) -> p i t", i=IT)
        results = [xnT[:, :, :].rearrange("p k (t c) -> p (k t) c", c=C), xn]

        names = ("loaded x_loaded setup_done ln_done std_ready sqrt_done prep_mm prep_freed hi_done mid_done "
                 "split_done scr0 scr1 scr2 scr3 stack0 stack1 stack2 v_ready qk_done exp_done pv_done max_mm max_red "
                 "m_all m_hi m_split rows_tr rows_ready o_evac norm_mm rsum_ready y_parts y_done y_tokens dve_chain "
                 "pool_chain tail_mm tail_freed x2_ready tanh_done logits_mm gap_ready exp2_done "
                 "rows_out took_ready counts_mm counts_out lane_ready table_mm table_out "
                 "shared_load routed_load route_load up_mm silu_done h_done down_mm acc_done gathered0 gathered1 turned xT_ready "
                 "up2_mm silu2_done h2_done h_turned hT_ready down2_mm y_ready scattered back0 back1 back2 back3 first_in stored routed").split()
        S = {n: sem(n) for n in names}
        scr = [S[f"scr{i}"] for i in range(NB)]
        stack = [S[f"stack{i}"] for i in range(NR)]
        gathered = [S["gathered0"], S["gathered1"]]
        back_in = [S[f"back{b}"] for b in range(B)]
        block = ctx.enter_context(nc.Block())

        weight_loads = [
            (ident[:, :], a["ident"]), (masks, a["masks"]), (sel[:, :], a["sel"]), (desc[:, :], a["desc"]),
            (wq[:, 0], a["Wq"].rearrange("(k p) c -> p k c", p=P)),
            (wq[:, 1], a["Wcq"].rearrange("(k p) c -> p k c", p=P)),
            (wq[:, 2], a["Wk"].rearrange("(k p) c -> p k c", p=P)),
            (wck, a["Wck"]), (wv, a["Wv"].rearrange("(k p) c -> p k c", p=P)),
            (wcv, a["Wcv"]), (wp[:, :, :], a["Wp"].rearrange("(k p) c -> p k c", p=P)),
            (bqk[:, :, :], a["bqk"]), (bv[:, :, :], a["bvp"]), (gates[:, :], a["gates"]),
            (wr[:, :, :], a["wrT"].rearrange("(k p) e -> p k e", p=P)), (rb[:, :], a["rb"]),
            (ctxT, a["ctxT"]),
        ]
        LOADED = 16 * len(weight_loads)

        pieces = []
        for b in range(B):
            pieces += [("turn", b, k) for k in range(2)]
            pieces += [("split", b, t, hf, 0, T) for t in range(3) for hf in range(2)]
            pieces += [("split", b, 3, hf, c0, c1) for hf in range(2) for c0, c1 in PREP_CHUNKS]
            pieces += [("value", b, t) for t in range(VT)]
        split_of = {}
        for n, p in enumerate(pieces):
            if p[0] == "split":
                split_of[n] = len(split_of)
        NSPLIT = len(split_of)
        turn_end = {b: 1 + max(n for n, p in enumerate(pieces) if p[:2] == ("turn", b)) for b in range(B)}

        def scratch(b, t, hf, part, c0, c1):
            dst, at = ((q_parts, 0), (q_parts, T), (k_parts, 0), (k_parts, T))[t]
            row = part if t < 2 else 2 - part
            u0 = b * H + hf * (H // 2)
            return dst[u0:u0 + H // 2, row * D:(row + 1) * D, at + c0:at + c1]

        @block.sync
        def _(sp):
            sp.dma_start(x[:, :, :], a["x"].rearrange("(t p) c -> p t c", p=P)).then_inc(S["x_loaded"], 16)
            for dst, src in weight_loads:
                sp.dma_start(dst, src).then_inc(S["loaded"], 16)
            for n, p in enumerate(pieces):
                if p[0] != "split":
                    continue
                _, b, t, hf, c0, c1 = p
                s = split_of[n]
                sp.wait_ge(S["split_done"], s + 1)
                for part, buf in enumerate((hi, mid, lo)):
                    sp.dma_start(scratch(b, t, hf, part, c0, c1), buf[:, s % NB, 0:c1 - c0]).then_inc(scr[s % NB], 16)
            for i in range(NB):
                sp.wait_ge(scr[i], 48 * len(range(i, NSPLIT, NB)))

            def stack_loads(u, r):
                for d0, d1 in ((0, 48), (48, 80), (80, 96)):
                    n = d1 - d0
                    sp.dma_start(qst[d0:d1, r, :, :].rearrange("p i t -> p (i t)"),
                                 q_parts[bass.ds(u, 1), 0:n, :].rearrange("a r t -> (a r) t")).then_inc(stack[r], 16)
                    sp.dma_start(kst[d0:d1, r, 0:T + TC],
                                 k_parts[bass.ds(u, 1), 48 - n:48, :].rearrange("a r t -> (a r) t")).then_inc(stack[r], 16)

            sp.wait_ge(S["pool_chain"], 6)
            for r in range(NR):
                stack_loads(r, r)
            with sp.Fori(0, NU // NR - 1) as i:
                for r in range(NR):
                    sp.wait_ge(S["qk_done"], i * (NR * NG) + NG * (r + 1))
                    stack_loads(i * NR + (NR + r), r)
            sp.wait_ge(S["qk_done"], (NU - NR) * NG)
            stack_loads(NU - 1, (NU - 1) % NR)

            sp.wait_ge(S["pv_done"], NU * NPV)
            sp.dma_start(weights[:, SHARED, :], a["experts"][SHARED]).then_inc(S["shared_load"], 16)
            sp.dma_start(rconst, a["route"]).then_inc(S["route_load"], 16)
            held = [e for e in range(NE) if e * WE < place["big"][0] + NT * C and (e + 1) * WE > place["big"][0]]
            for e in range(NE - 1):
                if e not in held:
                    sp.dma_start(weights[:, e, :], a["experts"][e]).then_inc(S["routed_load"], 16)
            sp.wait_ge(S["tail_mm"], 8)
            for e in held:
                sp.dma_start(weights[:, e, :], a["experts"][e]).then_inc(S["routed_load"], 16)
            for b in range(B):
                sp.wait_ge(S["ln_done"], NT + TT * (b + 1))
                sp.dma_start(xn_rows[b * T:(b + 1) * T].rearrange("(t p) c -> p t c", p=P),
                             xn[:, b * TT:(b + 1) * TT, :]).then_inc(S["rows_out"], 16)
            sp.wait_ge(S["routed"], 1)
            sp.dma_start(weights[:, NE - 1, :], a["experts"][NE - 1]).then_inc(S["routed_load"], 16)
            sp.wait_ge(S["scattered"], 16 * NSLOT)
            for b in range(B):
                for k in range(TOP):
                    r0 = k * NTOK + b * T
                    sp.dma_start(results[k][:, b * TT:(b + 1) * TT, :],
                                 y_rows[r0:r0 + T].rearrange("(t p) c -> p t c", p=P)).then_inc(back_in[b], 16)
            for b in range(B):
                sp.wait_ge(S["x2_ready"], NT + TT * (b + 1))
                sp.dma_start(a["out"].rearrange("(t p) c -> p t c", p=P)[:, b * TT:(b + 1) * TT, :],
                             x[:, b * TT:(b + 1) * TT, :]).then_inc(S["stored"], 16)
            sp.wait_ge(S["stored"], 16 * B)

        @block.tensor
        def _(pe):
            def layer_turn(bank, b, k):
                for t in range(TT):
                    mm = pe.transpose(bank[:, t * P:(t + 1) * P], xn[:, b * TT + t, k * P:(k + 1) * P], ident[:, :])
                return mm

            pe.wait_ge(S["loaded"], LOADED)
            for n, p in enumerate(pieces):
                bk = ps[:, n % 7, :]
                if n >= 7:
                    pe.wait_ge(S["prep_freed"], n - 6)
                b = p[1]
                if p[0] == "turn":
                    if n == 0:
                        pe.wait_ge(S["ln_done"], NT)
                    mm = layer_turn(bk, b, p[2])
                elif p[0] == "split":
                    _, _, t, hf, c0, c1 = p
                    pe.wait_ge(S["prep_freed"], turn_end[b])
                    if t < 3:
                        for k in range(2):
                            mm = pe.matmul(bk, wq[:, t, k, hf * P:(hf + 1) * P], xnT[:, k, b * T:(b + 1) * T],
                                           start=(k == 0), stop=(k == 1))
                    else:
                        mm = pe.matmul(bk[:, 0:c1 - c0], wck[:, hf * P:(hf + 1) * P],
                                       ctxT[:, b * TC + c0:b * TC + c1], start=True, stop=True)
                else:
                    t = p[2]
                    if t < TT:
                        for k in range(2):
                            mm = pe.matmul(bk[:, 0:C], xnT[:, k, b * T + t * P:b * T + (t + 1) * P], wv[:, k, :],
                                           start=(k == 0), stop=(k == 1))
                    else:
                        k0 = (t - TT) * P
                        kn = min(P, TC - k0)
                        mm = pe.matmul(bk[0:kn, 0:C], ctxT[:, b * TC + k0:b * TC + k0 + kn], wcv[:, :],
                                       start=True, stop=True)
                mm.then_inc(S["prep_mm"], 1)

            def max_piece(v, r, c):
                out = ps[:, 4 + c % 2, :]
                if not (isinstance(v, int) and v == 0 and c < 2):
                    pe.wait_ge(S["max_red"], v * NMAX + (c - 1))
                kind = MAX_PIECES[c][0]
                qx = qst[0:KROWS, r, 1, :]
                qs = qst[0:KROWS, r, 0, :]
                if kind == "cross":
                    _, qt, j = MAX_PIECES[c]
                    mm = pe.matmul(out, qx[:, qt * P:(qt + 1) * P],
                                   kst[0:KROWS, r, T + j * CHUNK:T + (j + 1) * CHUNK], start=True, stop=True)
                elif kind == "tail":
                    for qt in range(TT):
                        mm = pe.matmul(out[:, qt * TAIL:(qt + 1) * TAIL], qx[:, qt * P:(qt + 1) * P],
                                       kst[0:KROWS, r, T + NCH * CHUNK:T + TC], start=True, stop=True)
                elif kind == "pair":
                    for qt in range(2):
                        o = out[:, qt * 2 * P:(qt + 1) * 2 * P]
                        pe.matmul(o, qs[:, qt * P:(qt + 1) * P], kst[0:KROWS, r, 0:2 * P], start=True, stop=False)
                        mm = pe.matmul(o, identb[:, :], maskq[:, P - qt * P:3 * P - qt * P], start=False, stop=True)
                else:
                    qt = MAX_PIECES[c][1]
                    n = (qt + 1) * P
                    pe.matmul(out[:, 0:n], qs[:, qt * P:(qt + 1) * P], kst[0:KROWS, r, 0:n], start=True, stop=False)
                    mm = pe.matmul(out[:, n - P:n], identb[:, :], maskq[:, P:2 * P], start=False, stop=True)
                mm.then_inc(S["max_mm"], 1)

            def score(u, r, g, i):
                cross, kt, c0 = GROUPS[g][i]
                bk = ps[:, 2 * (g % 2) + c0 // 512, :]
                o0 = c0 % 512
                w = width(cross, kt)
                if cross:
                    mm = pe.matmul(bk[:, 0:w], kst[0:KROWS + MROWS, r, T + kt * P:T + (kt + 1) * P],
                                   qst[0:KROWS + MROWS, r, 1, :], start=True, stop=True)
                else:
                    pe.matmul(bk[:, o0:o0 + w], kst[0:KROWS + MROWS, r, kt * P:(kt + 1) * P],
                              qst[0:KROWS + MROWS, r, 0, kt * P:T], start=True, stop=False)
                    mm = pe.matmul(bk[:, o0:o0 + P], identb[:, :], maskk[:, :], start=False, stop=True)
                if i == len(GROUPS[g]) - 1:
                    mm.then_inc(S["qk_done"], 1)

            def values(u, r, i):
                batch, half = divmod(i, 2)
                pe.wait_ge(S["exp_done"], u * NG + (AFTER[batch] + 1))
                for cross, kt in BATCHES[batch]:
                    first = 0 if cross else kt * P
                    a0, a1 = max(first, half * T // 2), (half + 1) * T // 2
                    kn = CTAIL if cross and kt == CT - 1 else P
                    tiles = [(kt % 3 if cross else 3, a0, a1)]
                    if cross and kt == CT - 1:
                        tiles = [(q, a0 + 86 * q, min(a1, a0 + 86 * (q + 1))) for q in range(3)]
                    for q, b0, b1 in tiles:
                        if b0 >= b1:
                            continue
                        c0 = WHERE[cross, kt] + b0 - first
                        mm = pe.matmul(ps[32 * q:32 * q + VW, 6, b0:b1], vst[0:kn, r, TT + kt if cross else kt, :],
                                       pr[0:kn, c0:c0 + b1 - b0],
                                       start=(batch == 0 and half == 0), stop=(batch == len(BATCHES) - 1),
                                       skip_group_check=True)
                mm.then_inc(S["pv_done"], 1)

            def max_rows(v):
                pe.wait_ge(S["m_split"], v + 1)
                for i in range(2):
                    for t in range(TT):
                        r = 64 + 32 * i
                        mm = pe.matmul(ps7[r:r + MROWS, t * P:(t + 1) * P], mparts[:, i, t, :], identb[:, :],
                                       start=True, stop=True)
                mm.then_inc(S["rows_tr"], 1)

            def step(u, r, prev, nxt, nxt2):
                for item in PE_ORDER:
                    if item[0] == "score":
                        g = item[1]
                        if item[2] == 0:
                            if g == 0:
                                pe.wait_ge(S["rows_ready"], u * 2 + 2)
                            if prev or g >= 2:
                                pe.wait_ge(S["exp_done"], u * NG + (g - 1))
                        score(u, r, g, item[2])
                    elif item[0] == "values":
                        if item[1] < 0 and prev:
                            values(u - 1, (r - 1) % NR, NPV + item[1])
                        elif item[1] >= 0:
                            if item[1] == 0:
                                pe.wait_ge(S["v_ready"], u + 1)
                                if prev:
                                    pe.wait_ge(S["o_evac"], u)
                            values(u, r, item[1])
                    elif item[0] == "norm" and prev:
                        norm(u)
                    elif item[0] == "rows" and nxt:
                        if prev:
                            pe.wait_ge(S["y_parts"], u)
                        max_rows(u + 1)
                    elif item[0] == "max":
                        c = item[1]
                        if c < HALF and nxt:
                            max_piece(u + 1, (r + 1) % NR, c + HALF)
                        elif c >= HALF and nxt2:
                            if c == HALF:
                                r2 = (r + 2) % NR
                                pe.wait_ge(stack[r2], (u + 2 - r2) * 32 + 96)
                            max_piece(u + 2, (r + 2) % NR, c - HALF)

            def norm(u):
                for t in range(TT):
                    mm = pe.matmul(ps7[:, t * 2 * NSEL:(t + 1) * 2 * NSEL], osb[:, t * P:(t + 1) * P], sel[:, :],
                                   start=True, stop=True)
                mm.then_inc(S["norm_mm"], 1)

            pe.wait_ge(S["prep_freed"], len(pieces))
            pe.wait_ge(S["pool_chain"], 6)
            pe.wait_ge(S["setup_done"], 1)
            pe.wait_ge(stack[0], 96)
            for c in range(NMAX):
                max_piece(0, 0, c)
            pe.wait_ge(stack[1], 96)
            for c in range(HALF):
                max_piece(1, 1, c)
            max_rows(0)
            run_steps(pe, step)
            for i in range(3):
                values(NU - 1, (NU - 1) % NR, NPV - 3 + i)
            pe.wait_ge(S["o_evac"], NU)
            pe.wait_ge(S["y_parts"], NU - 1)
            norm(NU)

            pe.wait_ge(S["y_tokens"], B)
            for n in range(8):
                b, k = divmod(n, 2)
                bk = ps[:, n % 4, :]
                if n >= 4:
                    pe.wait_ge(S["tail_freed"], n - 3)
                for t in range(TT):
                    mm = pe.transpose(bk[:, t * P:(t + 1) * P], ytok[:, b * TT + t, k * P:(k + 1) * P], ident[:, :])
                mm.then_inc(S["tail_mm"], 1)
            for t in range(NT):
                bk = ps[:, 4 + t % 2, 0:C]
                pe.wait_ge(S["tail_freed"], 8 if t < 2 else 8 + t - 1)
                for k in range(2):
                    mm = pe.matmul(bk, xnT[:, k, t * P:(t + 1) * P], wp[:, k, :], start=(k == 0), stop=(k == 1))
                mm.then_inc(S["tail_mm"], 1)
            pe.wait_ge(S["ln_done"], 2 * NT)
            for n in range(8):
                b, k = divmod(n, 2)
                if n >= 4:
                    pe.wait_ge(S["tail_freed"], 8 + NT + n - 3)
                layer_turn(ps[:, n % 4, :], b, k).then_inc(S["tail_mm"], 1)
            pe.wait_ge(S["tail_freed"], 16 + NT)
            for t in range(NT):
                for k in range(2):
                    mm = pe.matmul(ps7[:, t * E8:t * E8 + NE], xnT[:, k, t * P:(t + 1) * P], wr[:, k, :],
                                   start=(k == 0), stop=(k == 1))
            mm.then_inc(S["logits_mm"], 1)

            def shared_up(tb):
                for it, (i0, m) in enumerate(CUTS):
                    k0 = tb * IT + it
                    if k0 >= 2:
                        pe.wait_ge(S["h_done"], k0 - 1)
                    for j, w in enumerate((wgs, wus)):
                        for k in range(2):
                            mm = pe.matmul(ps[0:m, 2 * (k0 % 2) + j, :], w[:, k, i0:i0 + m],
                                           xnT[:, k, tb * T:(tb + 1) * T], start=(k == 0), stop=(k == 1))
                    mm.then_inc(S["up_mm"], 1)

            def shared_down(tb):
                if tb:
                    pe.wait_ge(S["acc_done"], tb)
                pe.wait_ge(S["h_done"], (tb + 1) * IT)
                for t in range(TT):
                    out = ps[:, 4 + t // 2, (t % 2) * C:(t % 2 + 1) * C]
                    for it, (i0, m) in enumerate(CUTS):
                        mm = pe.matmul(out, hT[tb % 2][0:m, it, t * P:(t + 1) * P], wds[0:m, it, :],
                                       start=(it == 0), stop=(it == IT - 1))
                mm.then_inc(S["down_mm"], 1)

            def count_tokens():
                pe.wait_ge(S["took_ready"], 1)
                flat = took.rearrange("p t e -> p (t e)")
                out = ps[:, 6, :]
                pe.matmul(out[:, 0:NT * E8], before, flat, start=True, stop=False, skip_group_check=True)
                for j in range(1, NT):
                    pe.matmul(out[:, j * E8:NT * E8], ones, flat[:, 0:(NT - j) * E8], start=False, stop=(j == NT - 1),
                              skip_group_check=True)
                for t in range(NT):
                    mm = pe.matmul(out[:, NT * E8:(NT + 1) * E8], ones, took[:, t, :], start=(t == 0), stop=(t == NT - 1),
                                   skip_group_check=True)
                mm.then_inc(S["counts_mm"], 1)

            def fill_table(c):
                for n in range(4 * c, 4 * c + 4):
                    pe.wait_ge(S["lane_ready"], n + 1)
                    for j in range(4):
                        mm = pe.matmul(ps7[:, 0:NSLOT], in_lane[:, n % 2, j, :], row_in[:, 4 * (n % 4) + j, :],
                                       start=(n + j == 0), stop=(n == 7 and j == 3), skip_group_check=True)
                    mm.then_inc(S["table_mm"], 1)

            def turn_rows(i, b, bank=5):
                pe.wait_ge(gathered[b], (i - b) * 8 + 16)
                for k in range(2):
                    mm = pe.transpose(ps[:, bank, k * P:(k + 1) * P], xg[:, b, k * P:(k + 1) * P], ident[:, :])
                mm.then_inc(S["turned"], 1)

            def up(i, b, e):
                pe.wait_ge(S["xT_ready"], i + 1)
                for c in range(2):
                    for j in range(2):
                        for k in range(2):
                            o = (2 * j + k) * I + c * CH
                            mm = pe.matmul(ps[:, 2 * c + j, 0:CH], xgT[:, b, k, :], weights[:, bass.ds(e, 1), o:o + CH],
                                           start=(k == 0), stop=(k == 1))
                    mm.then_inc(S["up2_mm"], 1)

            def down(i, e):
                pe.wait_ge(S["hT_ready"], i * 2 + 2)
                if not (isinstance(i, int) and i == 0):
                    pe.wait_ge(S["y_ready"], i)
                for it, (i0, m) in enumerate(CUTS):
                    o = 4 * I + it * C
                    mm = pe.matmul(ps[:, 4, 0:C], hidT[0:m, it, :], weights[0:m, bass.ds(e, 1), o:o + C],
                                   start=(it == 0), stop=(it == IT - 1))
                mm.then_inc(S["down2_mm"], 1)

            def turn_hidden(i):
                for c in range(2):
                    pe.wait_ge(S["h2_done"], i * 2 + (c + 1))
                    bank = ps[:, 6, :] if c == 0 else ps7
                    for n, (i0, m) in enumerate(CUTS[3 * c:3 * c + 3]):
                        mm = pe.transpose(bank[0:m, n * P:(n + 1) * P], hid[:, c, i0 - c * CH:i0 - c * CH + m], ident[:, :])
                    mm.then_inc(S["h_turned"], 1)

            def expert_of(i):
                return pe.value_load(tile_expert[0:1, bass.ds(i, 1)], min_val=0, max_val=NE - 1)

            def turn(i, b, last):
                up(i, b, expert_of(i))
                down(i - 1, expert_of(i - 1))
                if not last:
                    turn_rows(i + 1, 1 - b)
                turn_hidden(i)

            pe.wait_ge(S["shared_load"], 16)
            shared_up(0)
            pe.wait_ge(S["route_load"], 16)
            count_tokens()
            shared_up(1)
            shared_down(0)
            fill_table(0)
            shared_up(2)
            shared_down(1)
            fill_table(1)
            shared_up(3)
            shared_down(2)
            turn_rows(0, 0, bank=6)
            shared_down(3)
            pe.wait_ge(S["routed_load"], 16 * NE)
            up(0, 0, expert_of(0))
            pe.wait_ge(S["acc_done"], B)
            turn_rows(1, 1)
            turn_hidden(0)
            with pe.Fori(0, NSLOT // 2 - 1) as i:
                turn(i * 2 + 1, 1, False)
                turn(i * 2 + 2, 0, False)
            turn(NSLOT - 1, 1, True)
            down(NSLOT - 1, expert_of(NSLOT - 1))

        @block.scalar
        def _(act):
            act.wait_ge(S["std_ready"], 1)
            act.activation(sd[:, :], sd[:, :], ACT.Sqrt).then_inc(S["sqrt_done"], 1)
            for n, p in enumerate(pieces):
                if p[0] != "split":
                    continue
                _, b, t, hf, c0, c1 = p
                s = split_of[n]
                act.wait_ge(S["prep_mm"], n + 1)
                if s >= NB:
                    act.wait_ge(scr[s % NB], 48 * (s // NB))
                act.activation(hi[:, s % NB, 0:c1 - c0], ps[:, n % 7, 0:c1 - c0], ACT.Identity,
                               bias=bqk[:, t, hf:hf + 1]).then_inc(S["hi_done"], 1)

            def rows(v, r):
                act.wait_ge(S["rows_tr"], v + 1)
                for i in range(2):
                    p0 = 64 + 32 * i
                    act.activation(qst[KROWS:KROWS + MROWS, r, i, :], ps7[p0:p0 + MROWS, :], ACT.Copy
                                   ).then_inc(S["rows_ready"], 1)

            def sums_out(u):
                act.wait_ge(S["pv_done"], u * NPV)
                act.activation(osb[:, :], ps[:, 6, :], ACT.Copy).then_inc(S["o_evac"], 1)

            def step(u, r, prev, nxt, nxt2):
                for g in range(NG):
                    act.wait_ge(S["qk_done"], u * NG + (g + 1))
                    if prev or FREED[g] > 0:
                        act.wait_ge(S["pv_done"], u * NPV + FREED[g])
                    n = sum(width(c, kt) for c, kt, _ in GROUPS[g])
                    c0 = BUF_AT[BUFFER[g]]
                    act.activation(pr[:, c0:c0 + n],
                                   ps[:, 2 * (g % 2):2 * (g % 2) + 2, :].rearrange("p b n -> p (b n)")[:, 0:n],
                                   ACT.Exp, scale=SCALE).then_inc(S["exp_done"], 1)
                    if g == 2 and prev:
                        sums_out(u)
                    if g == 6 and nxt:
                        rows(u + 1, (r + 1) % NR)

            rows(0, 0)
            run_steps(act, step)
            sums_out(NU)
            act.activation(tg[:, :], gates[:, :], ACT.Tanh).then_inc(S["tanh_done"], 1)
            act.wait_ge(S["std_ready"], 2)
            act.activation(sd[:, :], sd[:, :], ACT.Sqrt).then_inc(S["sqrt_done"], 1)
            act.wait_ge(S["gap_ready"], 1)
            act.activation(e2[:, :], e2[:, :], ACT.Exp).then_inc(S["exp2_done"], 1)

            def shared_silu(tb):
                for it, (i0, m) in enumerate(CUTS):
                    k0 = tb * IT + it
                    act.wait_ge(S["up_mm"], k0 + 1)
                    if k0 >= 2:
                        act.wait_ge(S["h_done"], k0 - 1)
                    else:
                        act.wait_ge(S["rows_out"], 16 * B)
                    act.activation(sg[0:m, k0 % 2, :], ps[0:m, 2 * (k0 % 2), :], ACT.Silu).then_inc(S["silu_done"], 1)

            shared_silu(0)
            act.wait_ge(S["counts_mm"], 1)
            act.activation(counts.rearrange("p t e -> p (t e)"), ps[:, 6, 0:(NT + 1) * E8], ACT.Copy).then_inc(S["counts_out"], 1)
            shared_silu(1)
            shared_silu(2)
            act.wait_ge(S["table_mm"], 8)
            act.activation(table, ps7[:, 0:NSLOT], ACT.Copy).then_inc(S["table_out"], 1)
            shared_silu(3)

            def turn(i):
                for c in range(2):
                    act.wait_ge(S["up2_mm"], i * 2 + (c + 1))
                    act.activation(gate_s[:, c, :], ps[:, 2 * c, 0:CH], ACT.Silu).then_inc(S["silu2_done"], 1)
                for c in range(2):
                    act.wait_ge(S["h_turned"], i * 2 + (c + 1))
                    bank = ps[:, 6, :] if c == 0 else ps7
                    m = CUTS[2][1]
                    act.activation(hidT[:, 3 * c:3 * c + 2, :].rearrange("p i t -> p (i t)"), bank[:, 0:2 * P], ACT.Copy)
                    act.activation(hidT[0:m, 3 * c + 2, :], bank[0:m, 2 * P:3 * P], ACT.Copy).then_inc(S["hT_ready"], 1)

            turn(0)
            with act.Fori(1, NSLOT) as i:
                turn(i)

        @block.gpsimd
        def _(pool):
            pool.memset(v_all[:, :, VT - 1, :], 0.0).then_inc(S["pool_chain"], 1)
            pool.wait_ge(S["pool_chain"], 1)
            pool.memset(vst[:, :, :, D + 1:VW], 0.0).then_inc(S["pool_chain"], 1)
            pool.wait_ge(S["pool_chain"], 2)
            pool.memset(vst[:, :, :, D:D + 1], 1.0).then_inc(S["pool_chain"], 1)
            pool.wait_ge(S["pool_chain"], 3)
            pool.memset(kst[0:KROWS, :, T + TC:T + CPAD], 0.0).then_inc(S["pool_chain"], 1)
            pool.wait_ge(S["pool_chain"], 4)
            pool.memset(kst[KROWS:KROWS + MROWS, :, 0:T + TC], 1.0).then_inc(S["pool_chain"], 1)
            pool.wait_ge(S["pool_chain"], 5)
            pool.memset(kst[KROWS:KROWS + MROWS, :, T + TC:T + CPAD], 0.0).then_inc(S["pool_chain"], 1)
            pool.wait_ge(S["pool_chain"], 6)
            for n, p in enumerate(pieces):
                if p[0] != "split":
                    continue
                _, b, t, hf, c0, c1 = p
                s = split_of[n]
                w = c1 - c0
                pool.wait_ge(S["prep_freed"], n + 1)
                if s >= NB:
                    pool.wait_ge(scr[s % NB], 48 * (s // NB))
                if s:
                    pool.wait_ge(S["split_done"], s)
                pool.tensor_copy(mid[:, s % NB, 0:w], res[:, s % NB, 0:w]).then_inc(S["mid_done"], 1)
                pool.wait_ge(S["mid_done"], s + 1)
                pool.tensor_tensor(lo[:, s % NB, 0:w], res[:, s % NB, 0:w], mid[:, s % NB, 0:w],
                                   ALU.subtract).then_inc(S["split_done"], 1)

            def value_copy(v, r):
                src = v_all[:, bass.ds(v, 1), :, :]
                pool.tensor_copy(vst[:, r:r + 1, :, 0:D], src).then_inc(S["v_ready"], 1)

            def head_output(u):
                dst = y[:, bass.ds(u - 1, 1), :, :]
                pool.wait_ge(S["y_parts"], u)
                pool.tensor_tensor(dst, yb[:, 0:1, :, 0, :], yb[:, 0:1, :, 1, :], ALU.add).then_inc(S["y_done"], 1)

            def step(u, r, prev, nxt, nxt2):
                if nxt:
                    if prev:
                        pool.wait_ge(S["pv_done"], u * NPV)
                    value_copy(u + 1, (r + 1) % NR)
                    pool.wait_ge(S["v_ready"], u + 2)
                if prev:
                    head_output(u)
                    pool.wait_ge(S["y_done"], u)

            pool.wait_ge(S["prep_freed"], len(pieces))
            value_copy(0, 0)
            pool.wait_ge(S["v_ready"], 1)
            run_steps(pool, step)
            head_output(NU)

            def gather(i):
                if i >= 2:
                    pool.wait_ge(S["turned"], i - 1)
                pool.indirect_dma_start(out=xg[:, i % 2, :], out_offset=None, in_=xn_rows,
                                        in_offset=bass.IndirectOffsetOnAxis(slot_table[:, i, 0:1], 0)
                                        ).then_inc(gathered[i % 2], 16)

            def scatter(i):
                if i:
                    pool.wait_ge(S["scattered"], i * 16)
                pool.wait_ge(S["y_ready"], i + 1)
                pool.indirect_dma_start(out=y_rows, out_offset=bass.IndirectOffsetOnAxis(slot_table[:, i, 1:2], 0),
                                        in_=yt[:, i % 2, :], in_offset=None).then_inc(S["scattered"], 16)

            pool.wait_ge(S["rows_out"], 16 * B)
            pool.wait_ge(S["routed"], 1)
            gather(0)
            gather(1)
            for i in range(NSLOT):
                if i + 2 < NSLOT:
                    gather(i + 2)
                scatter(i)

        @block.vector
        def _(dve):
            chain = [0]

            def link(ins):
                chain[0] += 1
                ins.then_inc(S["dve_chain"], 1)
                dve.wait_ge(S["dve_chain"], chain[0])

            def layernorm(k):
                for t in range(NT):
                    link(dve.bn_stats(st[:, t, :], x[:, t, :]))
                    link(dve.bn_aggr(mv[:, t, :], st[:, t, :]))
                dve.tensor_scalar(sd[:, :], mv[:, :, 1], EPS, None, ALU.add).then_inc(S["std_ready"], 1)
                dve.wait_ge(S["sqrt_done"], k)
                link(dve.reciprocal(rs[:, :], sd[:, :]))
                for t in range(NT):
                    dve.tensor_scalar(xn[:, t, :], x[:, t, :], mv[:, t, 0:1], rs[:, t:t + 1],
                                      ALU.subtract, ALU.mult).then_inc(S["ln_done"], 1)

            dve.wait_ge(S["x_loaded"], 16)
            layernorm(1)
            dve.wait_ge(S["loaded"], LOADED)
            dve.tensor_copy(maskq[:, :], masks[:, 0:3 * P])
            dve.tensor_copy(maskk[:, :], masks[:, 3 * P:4 * P])
            dve.tensor_copy(identb[:, :], ident[:, :]).then_inc(S["setup_done"], 1)
            dve.wait_ge(S["pool_chain"], 1)
            for n, p in enumerate(pieces):
                bk = ps[:, n % 7, :]
                b = p[1]
                dve.wait_ge(S["prep_mm"], n + 1)
                if p[0] == "turn":
                    dve.tensor_copy(xnT[:, p[2], b * T:(b + 1) * T], bk).then_inc(S["prep_freed"], 1)
                elif p[0] == "split":
                    _, _, t, hf, c0, c1 = p
                    s = split_of[n]
                    dve.wait_ge(S["hi_done"], s + 1)
                    if s >= NB:
                        dve.wait_ge(S["split_done"], s - NB + 1)
                    dve.scalar_tensor_tensor(out=res[:, s % NB, 0:c1 - c0], in0=bk[:, 0:c1 - c0],
                                             scalar=bqk[:, t, hf:hf + 1], in1=hi[:, s % NB, 0:c1 - c0],
                                             op0=ALU.add, op1=ALU.subtract).then_inc(S["prep_freed"], 1)
                else:
                    t = p[2]
                    kn = CTAIL if t == VT - 1 else P
                    dve.tensor_tensor(v_all[0:kn, b * H:(b + 1) * H, t, :],
                                      bk[0:kn, 0:C].rearrange("p (h d) -> p h d", h=H),
                                      bv[0:kn, 0 if t < TT else 1, :].rearrange("p (h d) -> p h d", h=H),
                                      ALU.add).then_inc(S["prep_freed"], 1)

            def reduce_piece(v, c):
                out = ps[:, 4 + c % 2, :]
                piece = MAX_PIECES[c]
                dve.wait_ge(S["max_mm"], v * NMAX + (c + 1))
                if c == 0 and not (isinstance(v, int) and v == 0):
                    dve.wait_ge(S["m_all"], v)
                if piece[0] == "pair" and not (isinstance(v, int) and v == 0):
                    dve.wait_ge(S["m_split"], v)
                if piece[0] == "cross":
                    m = mx[:, piece[1], piece[2]:piece[2] + 1]
                elif piece[0] == "tail":
                    m, out = mx[:, :, NCH], out[:, 0:TT * TAIL].rearrange("p (q k) -> p q k", q=TT)
                elif piece[0] == "pair":
                    m, out = mneg[:, 0, 0:2], out.rearrange("p (q k) -> p q k", q=2)
                else:
                    m, out = mneg[:, 0, piece[1]:piece[1] + 1], out[:, 0:(piece[1] + 1) * P]
                dve.tensor_reduce(m, out, AX_X, ALU.max).then_inc(S["max_red"], 1)

            def max_parts(v, i):
                if i == 0:
                    dve.wait_ge(S["max_red"], v * NMAX + NMAX)
                    dve.tensor_reduce(mneg[:, 1, :], mx[:, :, :], AX_X, ALU.max).then_inc(S["m_all"], 1)
                if i == 1:
                    dve.wait_ge(S["m_all"], v + 1)
                    dve.tensor_scalar(mparts[:, :, :, 0], mneg[:, :, :], -1.0, None, ALU.mult).then_inc(S["m_hi"], 1)
                if i == 2:
                    dve.wait_ge(S["m_hi"], v + 1)
                    dve.scalar_tensor_tensor(out=mparts[:, :, :, 1], in0=mneg[:, :, :], scalar=-1.0,
                                             in1=mparts[:, :, :, 0], op0=ALU.mult, op1=ALU.subtract
                                             ).then_inc(S["m_split"], 1)

            def outputs(u, i):
                nm = ps7[:, 0:TT * 2 * NSEL].rearrange("p (t s d) -> p t s d", t=TT, s=2)
                if i == 0:
                    dve.wait_ge(S["norm_mm"], u)
                    dve.reciprocal(rsum[:, :, :], nm[:, :, :, D]).then_inc(S["rsum_ready"], 1)
                if i == 1:
                    dve.wait_ge(S["rsum_ready"], u)
                    if not (isinstance(u, int) and u == 1):
                        dve.wait_ge(S["y_done"], u - 1)
                    dve.tensor_tensor(yb[:, 0, :, :, :], nm[:, :, :, 0:D],
                                      rsum[:, :, :].unsqueeze(3).to_broadcast([P, TT, 2, D]), ALU.mult
                                      ).then_inc(S["y_parts"], 1)

            def step(u, r, prev, nxt, nxt2):
                for c in range(NMAX):
                    if c < HALF and nxt:
                        reduce_piece(u + 1, c + HALF)
                    elif c >= HALF and nxt2:
                        reduce_piece(u + 2, c - HALF)
                    if nxt and HALF - 1 <= c < HALF + 2:
                        max_parts(u + 1, c - HALF + 1)
                    if prev and OUTPUTS_AT <= c < OUTPUTS_AT + 2:
                        outputs(u, c - OUTPUTS_AT)

            dve.wait_ge(S["prep_freed"], len(pieces))
            for c in range(NMAX):
                reduce_piece(0, c)
            for i in range(3):
                max_parts(0, i)
            for c in range(HALF):
                reduce_piece(1, c)
            run_steps(dve, step)
            for i in range(2):
                outputs(NU, i)

            dve.wait_ge(S["tanh_done"], 1)
            dve.wait_ge(S["y_done"], NU)
            for b in range(B):
                dve.tensor_copy(ytok[:, b * TT:(b + 1) * TT, :].rearrange("p t (h d) -> p t h d", h=H),
                                y[:, b * H:(b + 1) * H, :, :].rearrange("p h t d -> p t h d")).then_inc(S["y_tokens"], 1)
            for n in range(8):
                b, k = divmod(n, 2)
                dve.wait_ge(S["tail_mm"], n + 1)
                dve.tensor_copy(xnT[:, k, b * T:(b + 1) * T], ps[:, n % 4, :]).then_inc(S["tail_freed"], 1)
            for t in range(NT):
                dve.wait_ge(S["tail_mm"], 9 + t)
                row = osb[:, (t % 2) * C:(t % 2 + 1) * C]
                if t >= 2:
                    dve.wait_ge(S["x2_ready"], t - 1)
                dve.tensor_tensor(row, ps[:, 4 + t % 2, 0:C], bv[:, 2, :], ALU.add).then_inc(S["tail_freed"], 1)
                dve.wait_ge(S["tail_freed"], 9 + t)
                dve.scalar_tensor_tensor(out=x[:, t, :], in0=row, scalar=tg[:, 0:1], in1=x[:, t, :],
                                         op0=ALU.mult, op1=ALU.add).then_inc(S["x2_ready"], 1)
            dve.wait_ge(S["x2_ready"], NT)
            layernorm(2)
            for n in range(8):
                b, k = divmod(n, 2)
                dve.wait_ge(S["tail_mm"], 9 + NT + n)
                dve.tensor_copy(xnT[:, k, b * T:(b + 1) * T], ps[:, n % 4, :]).then_inc(S["tail_freed"], 1)
            link(dve.memset(lg[:, :, NE:E8], -3e38))
            dve.wait_ge(S["logits_mm"], 1)
            link(dve.tensor_tensor(lg[:, :, 0:NE], ps7[:, 0:NT * E8].rearrange("p (t e) -> p t e", t=NT)[:, :, 0:NE],
                                   rb[:, 0:NE].unsqueeze(1).to_broadcast([P, NT, NE]), ALU.add))

            def first_largest(src, m, s):
                full = [P, NT, E8]
                link(dve.tensor_reduce(m[:, :], src[:, :, :], AX_X, ALU.max))
                link(dve.tensor_tensor(s[:, :, :], src[:, :, :], m[:, :].unsqueeze(2).to_broadcast(full), ALU.is_equal))
                link(dve.tensor_tensor(key[:, :, :], s[:, :, :], desc[:, :].unsqueeze(1).to_broadcast(full), ALU.mult))
                link(dve.tensor_reduce(km[:, :], key[:, :, :], AX_X, ALU.max))
                link(dve.tensor_tensor(s[:, :, :], key[:, :, :], km[:, :].unsqueeze(2).to_broadcast(full), ALU.is_equal))

            first_largest(lg, m1, s1)
            link(dve.scalar_tensor_tensor(out=lg[:, :, :], in0=s1[:, :, :], scalar=-3e38, in1=lg[:, :, :],
                                          op0=ALU.mult, op1=ALU.add))
            first_largest(lg, m2, s2)
            dve.tensor_tensor(took, s1, s2, ALU.add).then_inc(S["took_ready"], 1)
            dve.tensor_tensor(e2[:, :], m2[:, :], m1[:, :], ALU.subtract).then_inc(S["gap_ready"], 1)
            dve.wait_ge(S["exp2_done"], 1)
            link(dve.tensor_scalar(rd[:, :], e2[:, :], 1.0, None, ALU.add))
            link(dve.reciprocal(rd[:, :], rd[:, :]))
            link(dve.tensor_scalar(weight[:, 0, :], rd[:, :], tg[:, 1:2], None, ALU.mult))
            link(dve.tensor_tensor(weight[:, 1, :], weight[:, 0, :], e2[:, :], ALU.mult))

            def shared_hidden(tb):
                if tb == 1:
                    dve.wait_ge(S["rows_out"], 16 * B)
                if tb >= 2:
                    dve.wait_ge(S["down_mm"], tb - 1)
                for it, (i0, m) in enumerate(CUTS):
                    k0 = tb * IT + it
                    dve.wait_ge(S["silu_done"], k0 + 1)
                    dve.tensor_tensor(hT[tb % 2][0:m, it, :], sg[0:m, k0 % 2, :], ps[0:m, 2 * (k0 % 2) + 1, :],
                                      ALU.mult).then_inc(S["h_done"], 1)

            def shared_out(tb):
                dve.wait_ge(S["down_mm"], tb + 1)
                for t in range(TT):
                    n = tb * TT + t
                    ins = dve.scalar_tensor_tensor(out=x[:, n, :], in0=ps[:, 4 + t // 2, (t % 2) * C:(t % 2 + 1) * C],
                                                   scalar=tg[:, 1:2], in1=x[:, n, :], op0=ALU.mult, op1=ALU.add)
                ins.then_inc(S["acc_done"], 1)

            def first_slots():
                dve.wait_ge(S["counts_out"], 1)
                dve.wait_ge(S["route_load"], 16)
                full = [P, E8, NT]
                link(dve.tensor_tensor(passed, counts[:, NT, :].unsqueeze(2).to_broadcast(full),
                                       bounds.unsqueeze(1).to_broadcast(full), ALU.is_gt))
                link(dve.tensor_reduce(ntiles, passed, AX_X, ALU.add))
                link(dve.tensor_tensor(earlier, ntiles.unsqueeze(1).to_broadcast([P, E8, E8]),
                                       below.rearrange("p (a b) -> p a b", a=E8), ALU.mult))
                link(dve.tensor_reduce(start, earlier, AX_X, ALU.add))
                full = [P, NSLOT, NE - 1]
                link(dve.tensor_tensor(reached, tile_no.unsqueeze(2).to_broadcast(full),
                                       start[:, 1:NE].unsqueeze(1).to_broadcast(full), ALU.is_ge))
                link(dve.tensor_reduce(expert_no, reached, AX_X, ALU.add))
                link(dve.tensor_copy(tile_expert[:, :], expert_no))
                link(dve.tensor_scalar(start, start, float(P), None, ALU.mult))
                link(dve.tensor_tensor(at, counts[:, 0:NT, :], start.unsqueeze(1).to_broadcast([P, NT, E8]), ALU.add))
                for k, s in enumerate((s1, s2)):
                    link(dve.tensor_tensor(taken, s, at, ALU.mult))
                    link(dve.tensor_reduce(slot[:, k, :], taken, AX_X, ALU.add))

            def table_parts(k):
                full = [P, NT, NSLOT + 1]
                link(dve.tensor_tensor(from_tile, slot[:, k, :].unsqueeze(2).to_broadcast(full),
                                       tile_begin.unsqueeze(1).to_broadcast(full), ALU.is_ge))
                link(dve.tensor_reduce(slot_tile[:, k, :], from_tile[:, :, 1:NSLOT + 1], AX_X, ALU.add))
                link(dve.scalar_tensor_tensor(out=lane[:, k, :], in0=slot_tile[:, k, :], scalar=-float(P), in1=slot[:, k, :],
                                              op0=ALU.mult, op1=ALU.add))
                if k:
                    dve.wait_ge(S["table_mm"], 4)
                link(dve.tensor_tensor(row_in, from_tile[:, :, 0:NSLOT], from_tile[:, :, 1:NSLOT + 1], ALU.subtract))
                link(dve.tensor_tensor(row_in, row_in, result_row[:, k * NT:(k + 1) * NT].unsqueeze(2).to_broadcast(
                    [P, NT, NSLOT]), ALU.mult))
                full = [P, 4, P]
                for n in range(4):
                    g = 4 * k + n
                    if g >= 2:
                        dve.wait_ge(S["table_mm"], g - 1)
                    dve.tensor_tensor(in_lane[:, g % 2], slot_of.unsqueeze(1).to_broadcast(full),
                                      lane[:, k, 4 * n:4 * n + 4].unsqueeze(2).to_broadcast(full), ALU.is_equal
                                      ).then_inc(S["lane_ready"], 1)

            def finish_table():
                dve.wait_ge(S["table_out"], 1)
                link(dve.tensor_scalar(empty, table, 0.0, spare_row, ALU.is_equal, ALU.mult))
                link(dve.scalar_tensor_tensor(out=result_at, in0=table, scalar=-1.0, in1=empty, op0=ALU.add, op1=ALU.add))
                link(dve.tensor_copy(slot_table[:, :, 1], result_at))
                for k in range(TOP):
                    link(dve.tensor_scalar(back, result_at, float((k + 1) * NTOK), -float(NTOK), ALU.is_ge, ALU.mult))
                    link(dve.tensor_tensor(empty, result_at if k == 0 else empty, back, ALU.add))
                dve.tensor_copy(slot_table[:, :, 0], empty).then_inc(S["routed"], 1)

            def rows_turned(i, b, bank=5):
                dve.wait_ge(S["turned"], i + 1)
                dve.tensor_copy(xgT[:, b, :, :].rearrange("p k t -> p (k t)"), ps[:, bank, 0:2 * P]).then_inc(S["xT_ready"], 1)

            def hidden(i):
                for c in range(2):
                    dve.wait_ge(S["silu2_done"], i * 2 + (c + 1))
                    dve.tensor_tensor(hid[:, c, :], gate_s[:, c, :], ps[:, 2 * c + 1, 0:CH], ALU.mult).then_inc(S["h2_done"], 1)

            def result(i, b, first):
                if not first:
                    dve.wait_ge(S["scattered"], i * 16 - 16)
                dve.wait_ge(S["down2_mm"], i + 1)
                dve.tensor_copy(yt[:, b, :], ps[:, 4, 0:C]).then_inc(S["y_ready"], 1)

            def turn(i, b, first):
                hidden(i)
                result(i - 1, 1 - b, first)
                rows_turned(i + 1, 1 - b)

            shared_hidden(0)
            first_slots()
            shared_hidden(1)
            table_parts(0)
            shared_out(0)
            shared_hidden(2)
            table_parts(1)
            shared_out(1)
            finish_table()
            shared_hidden(3)
            shared_out(2)
            rows_turned(0, 0, bank=6)
            shared_out(3)
            hidden(0)
            rows_turned(1, 1)
            turn(1, 1, True)
            turn(2, 0, True)
            with dve.Fori(1, NSLOT // 2 - 1) as i:
                turn(i * 2 + 1, 1, False)
                turn(i * 2 + 2, 0, False)
            hidden(NSLOT - 1)
            result(NSLOT - 2, 0, False)
            result(NSLOT - 1, 1, False)

            dve.wait_ge(S["acc_done"], B)
            for b in range(B):
                dve.wait_ge(back_in[b], 32)
                for k in range(TOP):
                    for t in range(b * TT, (b + 1) * TT):
                        if k:
                            dve.wait_ge(S["first_in"], t + 1)
                        dve.scalar_tensor_tensor(out=x[:, t, :], in0=results[k][:, t, :], scalar=weight[:, k, t:t + 1],
                                                 in1=x[:, t, :], op0=ALU.mult, op1=ALU.add
                                                 ).then_inc(S["x2_ready" if k else "first_in"], 1)


def kernel(**inputs):
    import numpy as np
    import concourse.bacc as bacc
    from concourse.bass_utils import run_bass_kernel_spmd

    i = {k.replace("L0_xattn_", "").replace("L0_ffn_", ""): np.asarray(v) for k, v in inputs.items()}

    def over(v, n):
        return np.broadcast_to(v.reshape(1, n), (P, n))

    future = np.triu(np.full((P, P), LOW, np.float32), 1)
    masks = np.concatenate([np.zeros((P, P), np.float32), future, np.full((P, P), LOW, np.float32), future.T], axis=1)
    lane = np.arange(P).reshape(P, 1)
    rows = np.arange(TOP * NT).reshape(1, TOP * NT) * P
    route = np.concatenate([np.triu(np.ones((P, P)), 1), np.ones((P, P)), over(np.arange(P), P), over(np.arange(NT) * P, NT),
                            over(np.tril(np.ones((E8, E8)), -1), E8 * E8), over(np.arange(NSLOT), NSLOT),
                            over(np.arange(NSLOT + 1) * P, NSLOT + 1), rows + lane + 1, TOP * NTOK + lane + 1],
                           axis=1).astype(np.float32)

    def expert_weights(g, u, d):
        dn = np.zeros((P, IT, C), np.float32)
        for it, (i0, m) in enumerate(CUTS):
            dn[:m, it] = d.T[i0:i0 + m]
        up = [w.T.reshape(2, P, I).transpose(1, 0, 2).reshape(P, 2 * I) for w in (g, u)]
        return np.concatenate(up + [dn.reshape(P, IT * C)], axis=1)

    experts = [expert_weights(i["rg"][e], i["ru"][e], i["rd"][e]) for e in range(NE)]
    experts.append(expert_weights(i["sg"], i["su"], i["sd"]))
    sel = np.zeros((P, 2 * NSEL), np.float32)
    for q in range(4):
        for d in range(NSEL):
            sel[32 * q + d, (q == 3) * NSEL + d] = 1.0
    arrays = {
        "x": i["x"].reshape(B * T, C),
        "ctxT": i["ctx_512"].transpose(2, 0, 1).reshape(CC, B * TC),
        "Wq": i["Wq"], "Wcq": i["Wcq"], "Wk": i["Wk"], "Wck": i["Wck"], "Wv": i["Wv"], "Wcv": i["Wcv"], "Wp": i["Wp"],
        "bqk": np.stack([i[n].reshape(2, P).T for n in ("bq", "bcq", "bk", "bck")], axis=1),
        "bvp": np.stack([over(i[n], C) for n in ("bv", "bcv", "bp")], axis=1),
        "gates": np.concatenate([over(i["g_xattn"], 1), over(i["g_ffn"], 1)], axis=1),
        "wrT": i["wr"].T,
        "rb": np.concatenate([over(i["rb"], NE), np.zeros((P, 1), np.float32)], axis=1),
        "experts": np.stack(experts), "route": route,
        "ident": np.eye(P, dtype=np.float32), "masks": masks, "sel": sel,
        "desc": over(np.arange(E8, 0, -1).astype(np.float32), E8),
    }
    arrays = {k: np.ascontiguousarray(v) for k, v in arrays.items()}
    nc = bacc.Bacc("TRN2", target_bir_lowering=False, num_devices=1)
    aps = {k: nc.dram_tensor("in_" + k, v.shape, F32, kind="ExternalInput").ap() for k, v in arrays.items()}
    aps["out"] = nc.dram_tensor("out", (B * T, C), F32, kind="ExternalOutput").ap()
    program(nc, aps)
    r = run_bass_kernel_spmd(nc, [{"in_" + k: v for k, v in arrays.items()}], core_ids=[0])
    return r.results[0]["out"].reshape(B, T, C)
```

```python
from contextlib import ExitStack

import numpy as np
import concourse.bass as bass
from concourse import mybir

F32 = mybir.dt.float32
BF16 = mybir.dt.bfloat16
U32 = mybir.dt.uint32
ACT = mybir.ActivationFunctionType
ALU = mybir.AluOpType
AX_X = mybir.AxisListType.X

P = 128
B, T, C = 4, 512, 256
TC, CC = 1601, 128
H, D = 16, 16
NB = 4
NU = B * H
TT = T // P
NT = B * TT
CT = -(-TC // P)
CTAIL = TC - (CT - 1) * P
VT = TT + CT
NE, I = 7, 704
TOP = 2
E8 = NE + 1
CH = I // 2
CUTS = [(c * CH + i, min(P, CH - i)) for c in range(2) for i in range(0, CH, P)]
IT = len(CUTS)
WHOLE, REST = divmod(I, P)
SHARED_CUTS = [(i, min(P, I - i)) for i in range(0, I, P)]
assert len(SHARED_CUTS) == IT == WHOLE + 1 and 2 * REST == P
WE = 4 * I + IT * C
NTOK = B * T
NSLOT = (NTOK * TOP + NE * (P - 1)) // P
SHARED = NE
ROUTE_WIDTHS = [P, P, P, NT, E8 * E8, NSLOT, NSLOT + 1, NT, 1]
ROUTE_COLS = sum(ROUTE_WIDTHS)
ROUTE_AT = [(sum(ROUTE_WIDTHS[:i]), sum(ROUTE_WIDTHS[:i + 1])) for i in range(len(ROUTE_WIDTHS))]
SCALE = float(D) ** -0.5
EPS = 1e-5
LOW = -1e30
KROWS = 6 * D
MROWS = 2
VW = 32

CHUNK = 512
NCH = TC // CHUNK
TAIL = TC - NCH * CHUNK
MAX_PIECES = [("cross", qt, j) for qt in range(TT) for j in range(NCH)] + [("tail",), ("pair",), ("self", 2), ("self", 3)]
NMAX = len(MAX_PIECES)

X, Y = True, False
GROUPS = [[(X, 0, 0), (X, 1, 512)], [(X, 2, 0), (Y, 0, 512)], [(Y, 1, 0), (Y, 3, 384), (Y, 2, 512)],
          [(X, 3, 0), (X, 4, 512)], [(X, 5, 0), (X, 6, 512)], [(X, 7, 0), (X, 8, 512)],
          [(X, 9, 0), (X, 10, 512)], [(X, 11, 0), (X, 12, 512)]]
BUFFER = [0, 1, 2, 3, 4, 1, 5, 3]
BUF_AT = [0, 1024, 2048, 2816, 3840, 4864]
BUF_END = 5888
NG = len(GROUPS)
BATCHES = [[(X, 0), (X, 1), (X, 2), (Y, 0)], [(X, 3), (X, 4), (X, 5), (Y, 1)],
           [(X, 6), (X, 7), (X, 8), (Y, 2)], [(X, 9), (X, 10), (X, 11), (X, 12)]]
AFTER = [1, 4, 5, 7]
NPV = 2 * len(BATCHES)


def half_batch(i):
    batch, half = divmod(i, 2)
    out = []
    for cross, kt in BATCHES[batch]:
        first = 0 if cross else kt * P
        out.append((cross, kt, max(first, half * T // 2), (half + 1) * T // 2, first))
    if i == 2:
        out.append((Y, TT - 1, (TT - 1) * P, T, (TT - 1) * P))
    return [t for t in out if t[2] < t[3]]


MASKED = [(0, 1), (1, 2), (3, 2), (2, 2)]
NEEDS_MASKED = {0: 1, 2: 3, 5: 4}

FREED = [-6, -2, -2, 0, -2, 2, 0, 4]
WHERE = {(c, kt): BUF_AT[BUFFER[g]] + c0 for g, grp in enumerate(GROUPS) for c, kt, c0 in grp}
NR = 3
CPAD = CT * P


HALF = NMAX // 2
MAXED = NMAX + HALF
LN_SUMS_AT, LN_STD_AT, LN_ROWS_AT = [15, 20, 20, 20], [10, 15, 15, 15], [8, 11, 11, 11]


def schedule():
    out = []
    for g in range(NG):
        tiles = [("score", g, i) for i in range(len(GROUPS[g]))]
        out += tiles + [("max", 2 * g), ("values", g - 3)]
        if g == 4:
            out.append(("norm",))
        if g == 6:
            out.append(("rows",))
        out.append(("max", 2 * g + 1))
    return out


XN_BANK = [0, 1, 4, 5, 6, 4, 5, 6]
SCALE_LAG = 5
REST_AT = 6
OUTPUTS_AT = 10


def run_steps(eng, step):
    step(0, 0, False, True, True)
    step(1, 1, True, True, True)
    heads = 2 * NR
    turns = (NU - 2 - 2) // heads
    with eng.Fori(0, turns) as i:
        for h in range(heads):
            step(i * heads + (h + 2), (h + 2) % NR, True, True, True)
    for u in range(heads * turns + 2, NU):
        step(u, u % NR, True, u + 1 < NU, u + 2 < NU)


FIRST_AHEAD = 16
AHEAD = 10
TURN_AHEAD = 4
PREP_CHUNKS = [(0, 401), (401, 801), (801, 1201), (1201, 1601)]


def width(cross, kt):
    return T if cross else T - kt * P


PE_ORDER = schedule()


def program(nc, a):
    ctx = ExitStack()
    with ctx:
        def sb(name, shape, dt=F32):
            return ctx.enter_context(nc.sbuf_tensor(name, shape, dt))

        def sem(name):
            return ctx.enter_context(nc.semaphore(name))

        q_parts = nc.dram_tensor("q_parts", (NU, D, 3, 2 * T), BF16, kind="Internal").ap()
        k_parts = nc.dram_tensor("k_parts", (NU, D, 3, T + TC), BF16, kind="Internal").ap()

        xn_rows = nc.dram_tensor("xn_rows", (NTOK, C), F32, kind="Internal").ap()

        ps = ctx.enter_context(nc.psum_tensor("ps", [P, 7, 512], F32))
        ps7 = ctx.enter_context(nc.psum_tensor("ps7", [P, 512], F32))

        x = sb("x", [P, NT, C])
        xnT = sb("xnT", [P, 2, B * T])
        shared = sb("shared", [P, NT * C])
        xn = shared[:, :].rearrange("p (t c) -> p t c", t=NT)
        parts = [("values", NU * VT * D), ("big", B * TC), ("kst", NR * (T + CPAD) // 2), ("qst", NR * T),
                 ("vst", NR * VT * VW), ("wq", 6 * C), ("wck", C), ("wv", 2 * C), ("wcv", C), ("res", NB * 512)]
        place, end = {}, 0
        for part, n in parts:
            place[part] = (end, end + n)
            end += n
        arena = sb("arena", [P, max(end, (NE + 1) * WE)])

        def region(part):
            return arena[:, place[part][0]:place[part][1]]

        v_all = region("values").rearrange("p (u t d) -> p u t d", u=NU, t=VT)
        big = region("big")
        ctxT = big
        identb = sb("identb", [P, P], BF16)
        maskq = sb("maskq", [P, 2 * P], BF16)
        ident = sb("ident", [P, P])
        masks = region("qst")[:, 0:2 * P]
        wq = region("wq").rearrange("p (w k c) -> p w k c", w=3, k=2)
        wck = region("wck")
        wv = region("wv").rearrange("p (k c) -> p k c", k=2)
        wcv = region("wcv")
        wp = sb("wp", [P, 2, C])
        bqk = sb("bqk", [P, 4, 2])
        bv = sb("bv", [P, 3, C])
        gates = sb("gates", [P, 2])
        tg = sb("tg", [P, 2])
        wr = sb("wr", [P, 2, NE])
        rb = sb("rb", [P, E8])
        desc = sb("desc", [P, E8])
        st = sb("st", [P, NT, 6])
        mv = sb("mv", [P, NT, 2])
        sd = sb("sd", [P, NT])
        rs = sb("rs", [P, NT])
        work = sb("work", [P, 3 * 1024])
        cut = work[:, :].bitcast(BF16).rearrange("p (b i t) -> p b i t", b=NB, i=3)
        res = region("res").rearrange("p (b t) -> p b t", b=NB)
        qst = region("qst").bitcast(BF16).rearrange("p (r i t) -> p r i t", r=NR, i=2)
        kst = region("kst").bitcast(BF16).rearrange("p (r t) -> p r t", r=NR)
        vst = region("vst").rearrange("p (r t w) -> p r t w", r=NR, t=VT)
        pr = big[:, 0:BUF_END]
        mx = sb("mx", [P, TT, NCH + 1])
        mneg = sb("mneg", [P, 2, TT])
        mparts = sb("mparts", [P, 2, TT, MROWS], BF16)
        osb = work[:, 2 * T:3 * T]
        sums = sb("sums", [P, 2, TT, D + 1])
        rsum = sb("rsum", [P, 2, TT])
        yb = sb("yb", [P, 2, TT, D])
        router = sb("router", [P, 4 * NT * E8])
        lg, key, s1, s2 = [router[:, NT * E8 * i:NT * E8 * (i + 1)].rearrange("p (t e) -> p t e", t=NT)
                        for i in range(4)]
        wr_cols = yb.rearrange("p a b d -> p (a b d)")[:, 0:2 * VW].rearrange("p (k w) -> p k w", k=2)
        logit_rows = wp[:, :, :].rearrange("p k c -> p (k c)")
        took = key
        m1 = sb("m1", [P, NT])
        m2 = sb("m2", [P, NT])
        km = sb("km", [P, NT])
        e2 = sb("e2", [P, NT])
        rd = sb("rd", [P, NT])
        weight = sb("weight", [P, TOP, NT])
        tile_expert = sb("tile_expert", [P, NSLOT], U32)
        slot_table = sb("slot_table", [P, NSLOT, 2], U32)
        slot_weight = router[:, 0:NSLOT]
        rt_end = [(NE - 1) * WE]

        def rt(*shape):
            n = int(np.prod(shape))
            o = rt_end[0]
            rt_end[0] += n
            assert rt_end[0] <= NE * WE
            v = arena[:, o:o + n]
            if len(shape) == 2:
                v = v.rearrange("p (a b) -> p a b", a=shape[0])
            if len(shape) == 3:
                v = v.rearrange("p (a b c) -> p a b c", a=shape[0], b=shape[1])
            return v

        rconst = rt(ROUTE_COLS)
        before, ones, slot_of, bounds, below, tile_no, tile_begin, token_no, spare_row = [
            rconst[:, c0:c1] for c0, c1 in ROUTE_AT]
        counts = rt(NT, E8)
        ntiles = rt(E8)
        earlier = rt(E8, E8)
        start = rt(E8)
        expert_no = rt(NSLOT)
        at = rt(NT, E8)
        taken = rt(NT, E8)
        slot = rt(TOP, NT)
        slot_tile = rt(TOP, NT)
        lane = rt(TOP, NT)
        from_tile = rt(NT, NSLOT + 1)
        row_in = rt(NT, 2 * NSLOT)
        in_lane = rt(2, 4, P)
        lanes = in_lane.rearrange("p a b c -> p (a b c)")
        passed = lanes[:, 0:E8 * NT].rearrange("p (e t) -> p e t", e=E8)
        reached = lanes[:, E8 * NT:E8 * NT + NSLOT * (NE - 1)].rearrange("p (i e) -> p i e", i=NSLOT)
        LEAD = NT // 2
        running = lanes[:, 4 * P:4 * P + 2 * (LEAD + NT) * E8].rearrange("p (b t e) -> p b t e", b=2, t=LEAD + NT)
        table = rt(NSLOT)
        empty = rt(NSLOT)
        result_at = rt(NSLOT)
        back = rt(NSLOT)

        weights = arena[:, 0:(NE + 1) * WE].rearrange("p (e w) -> p e w", e=NE + 1)
        wgus = weights[:, SHARED, 0:4 * I].rearrange("p (k i) -> p k i", k=2)
        wds = weights[:, SHARED, 4 * I:WE].rearrange("p (i c) -> p i c", i=IT)
        sg = shared[:, 0:2 * T].rearrange("p (b t) -> p b t", b=2)
        hT = [work[:, :].rearrange("p (i t) -> p i t", i=IT),
              shared[:, 2 * T:2 * T + IT * T].rearrange("p (i t) -> p i t", i=IT)]
        xg = wp
        yt = bv
        xgT = work[:, 0:4 * P].rearrange("p (b k t) -> p b k t", b=2, k=2)
        gate_s = work[:, 4 * P:4 * P + I].rearrange("p (c i) -> p c i", c=2)
        hid = work[:, 4 * P + I:4 * P + 2 * I].rearrange("p (c i) -> p c i", c=2)
        hidT = work[:, 4 * P + 2 * I:4 * P + 2 * I + IT * P].rearrange("p (i t) -> p i t", i=IT)

        names = ("loaded first_load early late masks_load x_first seq1 seq2 seq3 setup_done ln_done std_ready sqrt_done prep_mm prep_freed hi_done mid_done "
                 "split_done scr0 scr1 scr2 scr3 stack0 stack1 stack2 v_ready qk_done exp_done pv_done max_mm max_red "
                 "m_all m_hi m_split rows_tr rows_ready masked o_evac rest_added norm_mm sums_in rsum_ready y_parts y_done  dve_chain "
                 "pool_chain y_turned y_freed proj_mm xn_turned xn_freed x2_ready tanh_done bias_gated x_biased wr_ready logits_mm logits_out logits_turned gap_ready exp2_done "
                 "first_rows rows_out took_ready counts_mm counts_out lane_ready table_mm table_out "
                 "shared_load routed_load route_load up_mm silu_done h_done down_mm acc_done gathered0 gathered1 turned xT_ready "
                 "up2_mm silu2_done h2_done h_turned hT_ready down2_mm y_ready scattered based routed").split()
        S = {n: sem(n) for n in names}
        scr = [S[f"scr{i}"] for i in range(NB)]
        stack = [S[f"stack{i}"] for i in range(NR)]
        sequence = [S["x_first"], S["seq1"], S["seq2"], S["seq3"]]
        gathered = [S["gathered0"], S["gathered1"]]
        block = ctx.enter_context(nc.Block())

        def sequences(b0, b1):
            return (x[:, b0 * TT:b1 * TT, :], a["x"][b0 * T:b1 * T].rearrange("(t p) c -> p t c", p=P))

        first_cols = PREP_CHUNKS[0][1]
        first_loads = [
            (wck, a["Wck"]), (wcv, a["Wcv"]), (ctxT[:, 0:first_cols], a["ctxT"][:, 0:first_cols]), (bqk[:, :, :], a["bqk"]),
        ]
        early_loads = [
            (bv[:, :, :], a["bvp"]), (ctxT[:, first_cols:TC], a["ctxT"][:, first_cols:TC]),
        ]
        weight_loads = [
            (ident[:, :], a["ident"]),
            (wq[:, 0], a["Wq"].rearrange("(k p) c -> p k c", p=P)),
            (wq[:, 1], a["Wcq"].rearrange("(k p) c -> p k c", p=P)),
            (wq[:, 2], a["Wk"].rearrange("(k p) c -> p k c", p=P)),
            (wv, a["Wv"].rearrange("(k p) c -> p k c", p=P)),
        ]
        mask_loads = [(masks, a["masks"]), (gates[:, :], a["gates"])]
        late_loads = [
            (wp[:, :, :], a["Wp"].rearrange("(k p) c -> p k c", p=P)),
            (wr[:, :, :], a["wrT"].rearrange("(k p) e -> p k e", p=P)), (rb[:, :], a["rb"]), (desc[:, :], a["desc"]),
        ]
        later_loads = []
        for b in range(1, B):
            later_loads.append((*sequences(b, b + 1), sequence[b]))
            for c0, c1 in ((b * TC, b * TC + TC // 2), (b * TC + TC // 2, (b + 1) * TC)):
                later_loads.append((ctxT[:, c0:c1], a["ctxT"][:, c0:c1], sequence[b]))
            if b == 1:
                later_loads += [(*load, S["masks_load"]) for load in mask_loads]
        later_loads += [(*load, S["late"]) for load in late_loads]
        LOAD_AFTER = [*range(5), *range(6, 6 + 2 * (len(later_loads) - 5), 2)]
        FIRST_LOADS, EARLY, LOADED, MASKS, LATE = [16 * len(l) for l in (
            first_loads, early_loads, weight_loads, mask_loads, late_loads)]

        def mixed(some, others):
            return [p for _, p in sorted([((i + 0.5) / len(l), p) for l in (some, others) for i, p in enumerate(l)])]

        contexts = [mixed([("split", b, 3, hf, c0, c1) for hf in range(2) for c0, c1 in PREP_CHUNKS],
                          [("value", b, t) for t in range(TT, VT)]) for b in range(B)]
        own = [mixed([("split", b, t, hf, 0, T) for t in range(3) for hf in range(2)],
                     [("value", b, t) for t in range(TT)]) for b in range(B)]
        turns = [[("turn", b, k) for k in range(2)] for b in range(B)]
        sections = [contexts[0][:FIRST_AHEAD] + turns[0] + contexts[0][FIRST_AHEAD:FIRST_AHEAD + TURN_AHEAD]]
        for b in range(B):
            rest = contexts[b][FIRST_AHEAD + TURN_AHEAD if b == 0 else AHEAD:] + (contexts[b + 1][:AHEAD] if b < B - 1 else [])
            section = mixed(rest, own[b])
            if b < B - 1:
                section = section[:-TURN_AHEAD] + turns[b + 1] + section[-TURN_AHEAD:]
            sections.append(section)
        pieces = sections[0] + sections[1] + sections[2] + mixed(
            sections[3] + sections[4], [("max", c // NMAX, c % NMAX) for c in range(MAXED)])
        split_of = {}
        for n, p in enumerate(pieces):
            if p[0] == "split":
                split_of[n] = len(split_of)
        NSPLIT = len(split_of)
        FIRST = 1 + max(s for n, s in split_of.items() if pieces[n][1] == 0)
        begin = [min(n for n, p in enumerate(pieces) if p[0] != "max" and p[1] == b) for b in range(B)]
        turn_end = {b: 1 + max(n for n, p in enumerate(pieces) if p[:2] == ("turn", b)) for b in range(B)}
        turn_at = [turn_end[b] - 2 for b in range(B)]
        ROWS_AT = pieces.index(("max", 0, NMAX - 1)) + 8
        REST_OF_FIRST = min(n for n, p in enumerate(pieces) if p[0] == "split" and p[4] >= first_cols
                            or p[0] == "value" and p[2] >= TT and (p[2] - TT + 1) * P > first_cols)
        SETUP = turn_end[1]

        BIAS_AT = []
        for n in split_of:
            if len(BIAS_AT) < NT and n > max(SETUP + 12, turn_at[len(BIAS_AT) // TT]):
                BIAS_AT.append(n)
        assert len(BIAS_AT) == NT

        def scratch(b, t, hf, c0, c1):
            dst, at = ((q_parts, 0), (q_parts, T), (k_parts, 0), (k_parts, T))[t]
            u0 = b * H + hf * (H // 2)
            return dst[u0:u0 + H // 2, :, :, at + c0:at + c1].rearrange("u d i c -> (u d) i c")

        def place_of(t):
            return (0, 1, 2) if t < 2 else (2, 1, 0)

        @block.sync
        def _(sp):
            for dst, src in first_loads:
                sp.dma_start(dst, src).then_inc(S["first_load"], 16)
            for dst, src in early_loads:
                sp.dma_start(dst, src).then_inc(S["early"], 16)
            dst, src = sequences(0, 1)
            sp.dma_start(dst, src).then_inc(S["x_first"], 16)
            for dst, src in weight_loads:
                sp.dma_start(dst, src).then_inc(S["loaded"], 16)

            RUNS = ((0, 48), (48, 80), (80, 96))

            def stack_load(u, r, run, q):
                d0, d1 = RUNS[run]
                n = (d1 - d0) // D
                if q:
                    dst = qst[d0:d1, r, :, :].rearrange("p i t -> p (i t)")
                    src = q_parts[bass.ds(u, 1), :, 0:n, :]
                else:
                    dst = kst[d0:d1, r, 0:T + TC]
                    src = k_parts[bass.ds(u, 1), :, 3 - n:3, :]
                sp.dma_start(dst, src.rearrange("a d i t -> (a i) d t")).then_inc(stack[r], 16)

            def stack_loads(u, r):
                for run in range(3):
                    stack_load(u, r, run, True)
                    stack_load(u, r, run, False)

            first_stacks = [(r, r, run, q) for r in range(NR) for run in range(3) for q in (True, False)]
            for n, p in enumerate(pieces):
                if p[0] != "split":
                    continue
                _, b, t, hf, c0, c1 = p
                s = split_of[n]
                i = s - (FIRST + NB)
                if i == 0:
                    for k in range(NB):
                        sp.wait_ge(scr[k], 16 * len(range(k, FIRST, NB)))
                    sp.wait_ge(S["pool_chain"], 6)
                    sp.wait_ge(S["setup_done"], 1)
                if 0 <= i < len(first_stacks):
                    stack_load(*first_stacks[i])
                sp.wait_ge(S["split_done"], s + 1)
                sp.dma_start(scratch(b, t, hf, c0, c1), cut[:, s % NB, :, 0:c1 - c0]).then_inc(scr[s % NB], 16)
                if s in LOAD_AFTER:
                    dst, src, landed = later_loads[LOAD_AFTER.index(s)]
                    sp.dma_start(dst, src).then_inc(landed, 16)
            for i in range(NB):
                sp.wait_ge(scr[i], 16 * len(range(i, NSPLIT, NB)))

            with sp.Fori(0, NU // NR - 1) as i:
                for r in range(NR):
                    sp.wait_ge(S["qk_done"], i * (NR * NG) + NG * (r + 1))
                    stack_loads(i * NR + (NR + r), r)
            sp.dma_start(weights[:, SHARED, :], a["experts"][SHARED]).then_inc(S["shared_load"], 16)
            sp.wait_ge(S["qk_done"], (NU - NR) * NG)
            stack_loads(NU - 1, (NU - 1) % NR)

            sp.wait_ge(S["pv_done"], NU * NPV)
            sp.dma_start(rconst, a["route"]).then_inc(S["route_load"], 16)
            for b in range(B):
                sp.dma_start(weights[:, b, :], a["experts"][b]).then_inc(S["routed_load"], 16)
                sp.wait_ge(S["ln_done"], NT + TT * (b + 1))
                sp.dma_start(xn_rows[b * T:(b + 1) * T].rearrange("(t p) c -> p t c", p=P),
                             xn[:, b * TT:(b + 1) * TT, :]).then_inc(S["rows_out" if b else "first_rows"], 16)
            sp.dma_start(a["out"][NTOK:NTOK + P], xn[:, NT - 1, :]).then_inc(S["rows_out"], 16)
            for e in range(B, NE - 1):
                sp.dma_start(weights[:, e, :], a["experts"][e]).then_inc(S["routed_load"], 16)
            sp.wait_ge(S["routed"], 1)
            sp.dma_start(weights[:, NE - 1, :], a["experts"][NE - 1]).then_inc(S["routed_load"], 16)
            for b in range(B):
                sp.wait_ge(S["acc_done"], b + 1)
                sp.dma_start(a["out"][b * T:(b + 1) * T].rearrange("(t p) c -> p t c", p=P),
                             x[:, b * TT:(b + 1) * TT, :]).then_inc(S["based"], 16)
            sp.wait_ge(S["based"], 16 * B)
            sp.wait_ge(S["scattered"], 16 * NSLOT)

        @block.tensor
        def _(pe):
            def layer_turn(bank, b, k):
                for t in range(TT):
                    mm = pe.transpose(bank[:, t * P:(t + 1) * P], xn[:, b * TT + t, k * P:(k + 1) * P], ident[:, :])
                return mm

            def max_product(v, r, c, out):
                kind = MAX_PIECES[c][0]
                qx = qst[0:KROWS, r, 1, :]
                qs = qst[0:KROWS, r, 0, :]
                if kind == "cross":
                    _, qt, j = MAX_PIECES[c]
                    mm = pe.matmul(out, qx[:, qt * P:(qt + 1) * P],
                                   kst[0:KROWS, r, T + j * CHUNK:T + (j + 1) * CHUNK], start=True, stop=True)
                elif kind == "tail":
                    for qt in range(TT):
                        mm = pe.matmul(out[:, qt * TAIL:(qt + 1) * TAIL], qx[:, qt * P:(qt + 1) * P],
                                       kst[0:KROWS, r, T + NCH * CHUNK:T + TC], start=True, stop=True)
                elif kind == "pair":
                    pe.matmul(out[:, 0:2 * P], identb[:, :], maskq[:, :], start=True, stop=False)
                    pe.matmul(out[:, 0:P], qs[:, 0:P], kst[0:KROWS, r, 0:P], start=False, stop=True)
                    pe.matmul(out[:, 2 * P:4 * P], qs[:, P:2 * P], kst[0:KROWS, r, 0:2 * P], start=True, stop=False)
                    mm = pe.matmul(out[:, 3 * P:4 * P], identb[:, :], maskq[:, 0:P], start=False, stop=True)
                else:
                    qt = MAX_PIECES[c][1]
                    n = (qt + 1) * P
                    pe.matmul(out[:, 0:n], qs[:, qt * P:(qt + 1) * P], kst[0:KROWS, r, 0:n], start=True, stop=False)
                    mm = pe.matmul(out[:, n - P:n], identb[:, :], maskq[:, 0:P], start=False, stop=True)
                return mm

            def max_piece(v, r, c):
                n = v * NMAX + (c - 1 - MAXED)
                if not (isinstance(n, int) and n <= 0):
                    pe.wait_ge(S["max_red"], n)
                max_product(v, r, c, ps[:, 4 + c % 2, :]).then_inc(S["max_mm"], 1)

            def max_rows(v):
                pe.wait_ge(S["m_split"], v + 1)
                for i in range(2):
                    for t in range(TT):
                        r = 64 + 32 * i
                        mm = pe.matmul(ps7[r:r + MROWS, t * P:(t + 1) * P], mparts[:, i, t, :], identb[:, :],
                                       start=True, stop=True)
                mm.then_inc(S["rows_tr"], 1)

            pe.wait_ge(S["first_load"], FIRST_LOADS)
            for n, p in enumerate(pieces):
                bk = ps[:, n % 7, :]
                if n >= 7:
                    pe.wait_ge(S["prep_freed"], n - 6)
                b = p[1]
                if n == REST_OF_FIRST:
                    pe.wait_ge(S["early"], EARLY)
                if n == ROWS_AT:
                    max_rows(0)
                if b > 0 and n == begin[b]:
                    pe.wait_ge(sequence[b], 48)
                if p[0] == "max":
                    _, v, c = p
                    if v == 0 and c == 0:
                        pe.wait_ge(S["pool_chain"], 6)
                        pe.wait_ge(S["setup_done"], 1)
                    if c == 0:
                        pe.wait_ge(stack[v], 96)
                    mm = max_product(v, v, c, bk)
                elif p[0] == "turn":
                    if p[2] == 0:
                        pe.wait_ge(S["loaded"], LOADED)
                        pe.wait_ge(S["ln_done"], TT * (b + 1))
                    mm = layer_turn(bk, b, p[2])
                elif p[0] == "split":
                    _, _, t, hf, c0, c1 = p
                    if t < 3:
                        pe.wait_ge(S["prep_freed"], turn_end[b])
                        for k in range(2):
                            mm = pe.matmul(bk, wq[:, t, k, hf * P:(hf + 1) * P], xnT[:, k, b * T:(b + 1) * T],
                                           start=(k == 0), stop=(k == 1))
                    else:
                        mm = pe.matmul(bk[:, 0:c1 - c0], wck[:, hf * P:(hf + 1) * P],
                                       ctxT[:, b * TC + c0:b * TC + c1], start=True, stop=True)
                else:
                    t = p[2]
                    if t < TT:
                        for k in range(2):
                            mm = pe.matmul(bk[:, 0:C], xnT[:, k, b * T + t * P:b * T + (t + 1) * P], wv[:, k, :],
                                           start=(k == 0), stop=(k == 1))
                    else:
                        k0 = (t - TT) * P
                        kn = min(P, TC - k0)
                        mm = pe.matmul(bk[0:kn, 0:C], ctxT[:, b * TC + k0:b * TC + k0 + kn], wcv[:, :],
                                       start=True, stop=True)
                mm.then_inc(S["prep_mm"], 1)

            def score(u, r, g, i):
                cross, kt, c0 = GROUPS[g][i]
                bk = ps[:, 2 * (g % 2) + c0 // 512, :]
                o0 = c0 % 512
                w = width(cross, kt)
                if cross:
                    mm = pe.matmul(bk[:, 0:w], kst[0:KROWS + MROWS, r, T + kt * P:T + (kt + 1) * P],
                                   qst[0:KROWS + MROWS, r, 1, :], start=True, stop=True)
                else:
                    mm = pe.matmul(bk[:, o0:o0 + w], kst[0:KROWS + MROWS, r, kt * P:(kt + 1) * P],
                                   qst[0:KROWS + MROWS, r, 0, kt * P:T], start=True, stop=True)
                if i == len(GROUPS[g]) - 1:
                    mm.then_inc(S["qk_done"], 1)

            def values(u, r, i):
                pe.wait_ge(S["exp_done"], u * NG + (AFTER[i // 2] + 1))
                if i in NEEDS_MASKED:
                    pe.wait_ge(S["masked"], u * TT + NEEDS_MASKED[i])
                for cross, kt, a0, a1, first in half_batch(i):
                    rest = cross and kt == CT - 1
                    kn = CTAIL if rest else P
                    q = 3 if rest or not cross else kt % 3
                    sums_of = (ps7 if rest else ps[:, 6, :])[32 * q:32 * q + VW, a0:a1]
                    c0 = WHERE[cross, kt] + a0 - first
                    mm = pe.matmul(sums_of, vst[0:kn, r, TT + kt if cross else kt, :], pr[0:kn, c0:c0 + a1 - a0],
                                   start=(i == 0 or rest), stop=(i >= NPV - 2), skip_group_check=True)
                mm.then_inc(S["pv_done"], 1)

            def step(u, r, prev, nxt, nxt2):
                for item in PE_ORDER:
                    if item[0] == "score":
                        g = item[1]
                        if item[2] == 0:
                            if g == 0:
                                pe.wait_ge(S["rows_ready"], u * 2 + 2)
                            if prev or g >= 2:
                                pe.wait_ge(S["exp_done"], u * NG + (g - 1))
                        score(u, r, g, item[2])
                    elif item[0] == "values":
                        if item[1] < 0 and prev:
                            values(u - 1, (r - 1) % NR, NPV + item[1])
                        elif item[1] >= 0:
                            if item[1] == 0:
                                pe.wait_ge(S["v_ready"], u + 1)
                                if prev:
                                    pe.wait_ge(S["o_evac"], u)
                            values(u, r, item[1])
                    elif item[0] == "norm" and prev:
                        norm(u)
                    elif item[0] == "rows" and nxt:
                        if prev:
                            pe.wait_ge(S["sums_in"], u)
                        max_rows(u + 1)
                    elif item[0] == "max":
                        c = item[1]
                        if c < HALF and nxt:
                            max_piece(u + 1, (r + 1) % NR, c + HALF)
                        elif c >= HALF and nxt2:
                            if c == HALF:
                                r2 = (r + 2) % NR
                                pe.wait_ge(stack[r2], (u + 2 - r2) * 32 + 96)
                            max_piece(u + 2, (r + 2) % NR, c - HALF)

            def norm(u):
                pe.wait_ge(S["rest_added"], u)
                for t in range(TT):
                    mm = pe.transpose(ps7[:, t * P:(t + 1) * P], osb[:, t * P:(t + 1) * P], ident[:, :])
                mm.then_inc(S["norm_mm"], 1)

            pe.wait_ge(S["prep_freed"], len(pieces))
            run_steps(pe, step)
            pe.wait_ge(S["sums_in"], NU - 1)
            for i in range(3):
                values(NU - 1, (NU - 1) % NR, NPV - 3 + i)
            norm(NU)

            def logits():
                pe.wait_ge(S["wr_ready"], 1)
                pe.wait_ge(S["xn_freed"], 2 * B)
                for k in range(2):
                    for b in range(B):
                        mm = pe.matmul(ps7[VW * b:VW * (b + 1), :], wr_cols[:, k, :], xnT[:, k, b * T:(b + 1) * T],
                                       start=(k == 0), stop=(k == 1), skip_group_check=True)
                mm.then_inc(S["logits_mm"], 1)

            def turn_logits():
                pe.wait_ge(S["logits_out"], 1)
                for t in range(TT):
                    mm = pe.transpose(ps7[:, t * P:(t + 1) * P], logit_rows[:, t * P:(t + 1) * P], ident[:, :])
                mm.then_inc(S["logits_turned"], 1)

            pe.wait_ge(S["late"], LATE)
            pe.wait_ge(S["y_done"], NU)
            for n in range(8):
                b, k = divmod(n, 2)
                if n >= 4:
                    pe.wait_ge(S["y_freed"], n - 3)
                layer_turn(ps[:, n % 4, :], b, k).then_inc(S["y_turned"], 1)

            def project(b):
                pe.wait_ge(S["y_freed"], 2 * b + 2)
                for t in range(b * TT, (b + 1) * TT):
                    bk = ps[:, 4 + t % 3, 0:C]
                    if t >= 3:
                        pe.wait_ge(S["x2_ready"], t - 2)
                    for k in range(2):
                        mm = pe.matmul(bk, xnT[:, k, t * P:(t + 1) * P], wp[:, k, :], start=(k == 0), stop=(k == 1))
                    mm.then_inc(S["proj_mm"], 1)

            def turn_xn(b):
                pe.wait_ge(S["ln_done"], NT + TT * (b + 1))
                if b == 0:
                    pe.wait_ge(S["y_freed"], 8)
                else:
                    pe.wait_ge(S["x2_ready"], NT)
                for k in range(2):
                    if XN_BANK.index(XN_BANK[2 * b + k]) < 2 * b + k:
                        pe.wait_ge(S["xn_freed"], 1 + XN_BANK.index(XN_BANK[2 * b + k]))
                    layer_turn(ps[:, XN_BANK[2 * b + k], :], b, k).then_inc(S["xn_turned"], 1)

            def shared_up(tb, it0=0, it1=IT):
                for it in range(it0, it1):
                    k0 = tb * IT + it
                    if k0 >= 2:
                        pe.wait_ge(S["h_done"], k0 - 1)
                    elif k0 == 0:
                        pe.wait_ge(S["xn_freed"], 2)
                    for j, w0 in enumerate((it * P, I + REST + it * P) if it < WHOLE else (it * P,)):
                        for k in range(2):
                            mm = pe.matmul(ps[:, 2 * (k0 % 2) + j, :], wgus[:, k, w0:w0 + P],
                                           xnT[:, k, tb * T:(tb + 1) * T], start=(k == 0), stop=(k == 1))
                    mm.then_inc(S["up_mm"], 1)

            def shared_down(tb, t0=0, t1=TT):
                if tb and t0 == 0:
                    pe.wait_ge(S["acc_done"], tb)
                pe.wait_ge(S["h_done"], (tb + 1) * IT)
                for t in range(t0, t1):
                    out = ps[:, 4 + t // 2, (t % 2) * C:(t % 2 + 1) * C]
                    for it, (i0, m) in enumerate(SHARED_CUTS):
                        mm = pe.matmul(out, hT[tb % 2][0:m, it, t * P:(t + 1) * P], wds[0:m, it, :],
                                       start=(it == 0), stop=(it == IT - 1))
                if t1 == TT:
                    mm.then_inc(S["down_mm"], 1)

            def count_tokens():
                pe.wait_ge(S["took_ready"], 1)
                flat = took.rearrange("p t e -> p (t e)")
                pe.matmul(ps[:, 6, 0:NT * E8], before, flat, start=True, stop=True)
                mm = pe.matmul(ps[:, 6, NT * E8:2 * NT * E8], ones, flat, start=True, stop=True)
                mm.then_inc(S["counts_mm"], 1)

            def fill_table(c):
                for n in range(4 * c, 4 * c + 4):
                    pe.wait_ge(S["lane_ready"], n + 1)
                    for j in range(4):
                        mm = pe.matmul(ps7[:, 0:2 * NSLOT], in_lane[:, n % 2, j, :], row_in[:, 4 * (n % 4) + j, :],
                                       start=(n + j == 0), stop=(n == 7 and j == 3), skip_group_check=True)
                    mm.then_inc(S["table_mm"], 1)

            def turn_rows(i, b, bank=5):
                pe.wait_ge(gathered[b], (i - b) * 8 + 16)
                for k in range(2):
                    mm = pe.transpose(ps[:, bank, k * P:(k + 1) * P], xg[:, b, k * P:(k + 1) * P], ident[:, :])
                mm.then_inc(S["turned"], 1)

            def up(i, b, e, c):
                if c == 0:
                    pe.wait_ge(S["xT_ready"], i + 1)
                for j in range(2):
                    for k in range(2):
                        o = (2 * j + k) * I + c * CH
                        mm = pe.matmul(ps[:, 2 * c + j, 0:CH], xgT[:, b, k, :], weights[:, bass.ds(e, 1), o:o + CH],
                                       start=(k == 0), stop=(k == 1))
                mm.then_inc(S["up2_mm"], 1)

            def down(i, e, half):
                if half == 0:
                    pe.wait_ge(S["hT_ready"], i * 2 + 2)
                    if not (isinstance(i, int) and i == 0):
                        pe.wait_ge(S["y_ready"], i)
                for it in range(half * IT // 2, (half + 1) * IT // 2):
                    m = CUTS[it][1]
                    o = 4 * I + it * C
                    mm = pe.matmul(ps[:, 4, 0:C], hidT[0:m, it, :], weights[0:m, bass.ds(e, 1), o:o + C],
                                   start=(it == 0), stop=(it == IT - 1))
                if half:
                    mm.then_inc(S["down2_mm"], 1)

            def turn_hidden(i):
                for c in range(2):
                    pe.wait_ge(S["h2_done"], i * 2 + (c + 1))
                    bank = ps[:, 6, :] if c == 0 else ps7
                    for n, (i0, m) in enumerate(CUTS[3 * c:3 * c + 3]):
                        mm = pe.transpose(bank[0:m, n * P:(n + 1) * P], hid[:, c, i0 - c * CH:i0 - c * CH + m], ident[:, :])
                    mm.then_inc(S["h_turned"], 1)

            def expert_of(i):
                return pe.value_load(tile_expert[0:1, bass.ds(i, 1)], min_val=0, max_val=NE - 1)

            def turn(i, b, e, e_before=None, ahead=True):
                up(i, b, e, 0)
                if e_before is None:
                    e_before = expert_of(i - 1)
                up(i, b, e, 1)
                if ahead:
                    turn_rows(i + 1, 1 - b)
                down(i - 1, e_before, 0)
                e_next = expert_of(i + 1) if ahead and b else None
                down(i - 1, e_before, 1)
                turn_hidden(i)
                return e_next

            for b in range(B):
                if b == B - 1:
                    turn_xn(0)
                project(b)
            pe.wait_ge(S["shared_load"], 16)
            shared_up(0)
            for b in range(1, B):
                turn_xn(b)
            shared_up(1, 0, 1)
            logits()
            shared_up(1, 1, 2)
            turn_logits()
            shared_up(1, 2, IT)
            pe.wait_ge(S["route_load"], 16)
            count_tokens()
            shared_down(0)
            shared_up(2)
            fill_table(0)
            shared_down(1)
            shared_up(3)
            fill_table(1)
            shared_down(2)
            shared_down(3, 0, TT // 2)
            turn_rows(0, 0, bank=6)
            shared_down(3, TT // 2, TT)
            pe.wait_ge(S["routed_load"], 16 * NE)
            e = expert_of(0)
            for c in range(2):
                up(0, 0, e, c)
            pe.wait_ge(S["acc_done"], B)
            turn_rows(1, 1)
            turn_hidden(0)
            with pe.Fori(0, NSLOT // 2 - 1) as i:
                e = expert_of(i * 2 + 1)
                e_next = turn(i * 2 + 1, 1, e)
                turn(i * 2 + 2, 0, e_next, e)
            e = expert_of(NSLOT - 1)
            turn(NSLOT - 1, 1, e, ahead=False)
            for half in range(2):
                down(NSLOT - 1, e, half)

        @block.scalar
        def _(act):
            def deviations(k, b0, b1):
                act.wait_ge(S["std_ready"], k)
                act.activation(sd[:, b0 * TT:b1 * TT], sd[:, b0 * TT:b1 * TT], ACT.Sqrt).then_inc(S["sqrt_done"], 1)

            def first_part(n):
                _, b, t, hf, c0, c1 = pieces[n]
                s = split_of[n]
                act.wait_ge(S["prep_mm"], n + 1)
                if s >= NB:
                    act.wait_ge(scr[s % NB], 16 * (s // NB))
                act.activation(cut[:, s % NB, place_of(t)[0], 0:c1 - c0], ps[:, n % 7, 0:c1 - c0], ACT.Identity,
                               bias=bqk[:, t, hf:hf + 1]).then_inc(S["hi_done"], 1)

            def second_part(n):
                _, b, t, hf, c0, c1 = pieces[n]
                s = split_of[n]
                act.wait_ge(S["prep_freed"], n + 1)
                act.activation(cut[:, s % NB, place_of(t)[1], 0:c1 - c0], res[:, s % NB, 0:c1 - c0], ACT.Copy
                               ).then_inc(S["mid_done"], 1)

            def rows(v, r):
                act.wait_ge(S["rows_tr"], v + 1)
                for i in range(2):
                    p0 = 64 + 32 * i
                    act.activation(qst[KROWS:KROWS + MROWS, r, i, :], ps7[p0:p0 + MROWS, :], ACT.Copy
                                   ).then_inc(S["rows_ready"], 1)

            act.wait_ge(S["first_load"], FIRST_LOADS)
            splits = sorted(split_of)
            first_part(splits[0])
            for n, n_next in zip(splits, splits[1:]):
                first_part(n_next)
                second_part(n)
                if n < ROWS_AT <= n_next:
                    rows(0, 0)
                for b in range(B):
                    if n < turn_at[b] - LN_STD_AT[b] <= n_next:
                        deviations(1 + b, b, b + 1)
                if n < SETUP + 7 <= n_next:
                    act.wait_ge(S["masks_load"], MASKS)
                    act.activation(tg[:, :], gates[:, :], ACT.Tanh).then_inc(S["tanh_done"], 1)
            second_part(splits[-1])

            def sums_out(u):
                act.wait_ge(S["pv_done"], u * NPV)
                act.activation(osb[:, :], ps[:, 6, :], ACT.Copy).then_inc(S["o_evac"], 1)

            def step(u, r, prev, nxt, nxt2):
                for g in range(NG):
                    act.wait_ge(S["qk_done"], u * NG + (g + 1))
                    if prev or FREED[g] > 0:
                        act.wait_ge(S["pv_done"], u * NPV + FREED[g])
                    n = sum(width(c, kt) for c, kt, _ in GROUPS[g])
                    c0 = BUF_AT[BUFFER[g]]
                    act.activation(pr[:, c0:c0 + n],
                                   ps[:, 2 * (g % 2):2 * (g % 2) + 2, :].rearrange("p b n -> p (b n)")[:, 0:n],
                                   ACT.Exp, scale=SCALE).then_inc(S["exp_done"], 1)
                    if g == 2 and prev:
                        if isinstance(u, int) and u == 1:
                            for i in range(NB):
                                act.wait_ge(scr[i], 16 * len(range(i, NSPLIT, NB)))
                        sums_out(u)
                    if g == 6 and nxt:
                        rows(u + 1, (r + 1) % NR)

            run_steps(act, step)
            sums_out(NU)
            for n in range(8):
                b, k = divmod(n, 2)
                act.wait_ge(S["y_turned"], n + 1)
                act.activation(xnT[:, k, b * T:(b + 1) * T], ps[:, n % 4, :], ACT.Copy).then_inc(S["y_freed"], 1)

            def xn_out(b):
                for n in (2 * b, 2 * b + 1):
                    act.wait_ge(S["xn_turned"], n + 1)
                    act.activation(xnT[:, n % 2, b * T:(b + 1) * T], ps[:, XN_BANK[n], :], ACT.Copy).then_inc(S["xn_freed"], 1)

            def shared_silu(tb, it0=0, it1=IT):
                for it, (i0, m) in [*enumerate(SHARED_CUTS)][it0:it1]:
                    k0 = tb * IT + it
                    act.wait_ge(S["up_mm"], k0 + 1)
                    if k0 >= 2:
                        act.wait_ge(S["h_done"], k0 - 1)
                    else:
                        act.wait_ge(S["first_rows"], 16)
                    act.activation(sg[0:m, k0 % 2, :], ps[0:m, 2 * (k0 % 2), :], ACT.Silu).then_inc(S["silu_done"], 1)

            deviations(1 + B, 0, 1)
            deviations(2 + B, 1, 2)
            xn_out(0)
            deviations(3 + B, 2, 3)
            deviations(4 + B, 3, 4)
            shared_silu(0)
            for b in range(1, B):
                xn_out(b)
            shared_silu(1, 0, 1)
            act.wait_ge(S["logits_mm"], 1)
            act.activation(logit_rows, ps7[:, :], ACT.Copy).then_inc(S["logits_out"], 1)
            shared_silu(1, 1, IT)
            act.wait_ge(S["gap_ready"], 1)
            act.activation(e2[:, :], e2[:, :], ACT.Exp).then_inc(S["exp2_done"], 1)
            act.wait_ge(S["counts_mm"], 1)
            act.activation(running[:, 0, LEAD:, :].rearrange("p t e -> p (t e)"), ps[:, 6, NT * E8:2 * NT * E8], ACT.Copy
                           ).then_inc(S["counts_out"], 1)
            shared_silu(2)
            shared_silu(3)
            act.wait_ge(S["table_mm"], 8)
            act.activation(table, ps7[:, 0:NSLOT], ACT.Copy)
            act.activation(slot_weight[:, :], ps7[:, NSLOT:2 * NSLOT], ACT.Copy).then_inc(S["table_out"], 1)

            def turn(i):
                for c in range(2):
                    act.wait_ge(S["up2_mm"], i * 2 + (c + 1))
                    act.activation(gate_s[:, c, :], ps[:, 2 * c, 0:CH], ACT.Silu).then_inc(S["silu2_done"], 1)
                for c in range(2):
                    act.wait_ge(S["h_turned"], i * 2 + (c + 1))
                    bank = ps[:, 6, :] if c == 0 else ps7
                    m = CUTS[2][1]
                    act.activation(hidT[:, 3 * c:3 * c + 2, :].rearrange("p i t -> p (i t)"), bank[:, 0:2 * P], ACT.Copy)
                    act.activation(hidT[0:m, 3 * c + 2, :], bank[0:m, 2 * P:3 * P], ACT.Copy).then_inc(S["hT_ready"], 1)

            turn(0)
            with act.Fori(1, NSLOT) as i:
                turn(i)

        @block.gpsimd
        def _(pool):
            pool.memset(v_all[:, :, VT - 1, :], 0.0).then_inc(S["pool_chain"], 1)
            pool.wait_ge(S["pool_chain"], 1)
            pool.memset(vst[:, :, :, D + 1:VW], 0.0).then_inc(S["pool_chain"], 1)
            pool.wait_ge(S["pool_chain"], 2)
            pool.memset(vst[:, :, :, D:D + 1], 1.0).then_inc(S["pool_chain"], 1)
            pool.wait_ge(S["pool_chain"], 3)
            pool.memset(kst[0:KROWS, :, T + TC:T + CPAD], 0.0).then_inc(S["pool_chain"], 1)
            pool.wait_ge(S["pool_chain"], 4)
            pool.memset(kst[KROWS:KROWS + MROWS, :, 0:T + TC], 1.0).then_inc(S["pool_chain"], 1)
            pool.wait_ge(S["pool_chain"], 5)
            pool.memset(kst[KROWS:KROWS + MROWS, :, T + TC:T + CPAD], 0.0).then_inc(S["pool_chain"], 1)
            pool.wait_ge(S["pool_chain"], 6)
            for n, p in enumerate(pieces):
                if p[0] != "split":
                    continue
                _, b, t, hf, c0, c1 = p
                s = split_of[n]
                w = c1 - c0
                if s:
                    pool.wait_ge(S["split_done"], s)
                pool.wait_ge(S["mid_done"], s + 1)
                pool.tensor_tensor(cut[:, s % NB, place_of(t)[2], 0:w], res[:, s % NB, 0:w],
                                   cut[:, s % NB, place_of(t)[1], 0:w], ALU.subtract).then_inc(S["split_done"], 1)
                if n in BIAS_AT:
                    tile = BIAS_AT.index(n)
                    pool.wait_ge(S["bias_gated"], 1)
                    pool.wait_ge(S["ln_done"], (tile // TT + 1) * TT)
                    pool.wait_ge(S["split_done"], s + 1)
                    pool.tensor_tensor(x[:, tile, :], x[:, tile, :], bv[:, 2, :], ALU.add).then_inc(S["x_biased"], 1)
                    pool.wait_ge(S["x_biased"], tile + 1)

            def value_copy(v, r):
                src = v_all[:, bass.ds(v, 1), :, :]
                pool.tensor_copy(vst[:, r:r + 1, :, 0:D], src).then_inc(S["v_ready"], 1)

            def head_output(u):
                v = u - 1
                dst = xn[:, bass.ds(v // H * TT, TT), bass.ds(v % H * D, D)]
                pool.wait_ge(S["rsum_ready"], u)
                pool.tensor_tensor(yb[:, :, :, :], sums[:, :, :, 0:D],
                                   rsum[:, :, :].unsqueeze(3).to_broadcast([P, 2, TT, D]), ALU.mult).then_inc(S["y_parts"], 1)
                pool.wait_ge(S["y_parts"], u)
                pool.tensor_tensor(dst, yb[:, 0, :, :], yb[:, 1, :, :], ALU.add).then_inc(S["y_done"], 1)

            def mask(u, n0, n1):
                for n in range(n0, n1):
                    kt, g = MASKED[n]
                    exps = pr[:, WHERE[Y, kt]:WHERE[Y, kt] + P]
                    pool.wait_ge(S["exp_done"], u * NG + (g + 1))
                    pool.nop(nofuse=True)
                    pool.affine_select(out=exps, in_=exps, pattern=[[1, P]], compare_op=ALU.is_ge, fill=0.0, base=0,
                                       channel_multiplier=-1).then_inc(S["masked"], 1)
                    pool.wait_ge(S["masked"], u * TT + (n + 1))

            def step(u, r, prev, nxt, nxt2):
                mask(u, 0, 1)
                if nxt:
                    if prev:
                        pool.wait_ge(S["pv_done"], u * NPV)
                    value_copy(u + 1, (r + 1) % NR)
                    pool.wait_ge(S["v_ready"], u + 2)
                mask(u, 1, TT)
                if prev:
                    head_output(u)
                    pool.wait_ge(S["y_done"], u)

            pool.wait_ge(S["prep_freed"], len(pieces))
            value_copy(0, 0)
            pool.wait_ge(S["v_ready"], 1)
            run_steps(pool, step)
            head_output(NU)

            def gather(i):
                if i >= 2:
                    pool.wait_ge(S["turned"], i - 1)
                pool.indirect_dma_start(out=xg[:, i % 2, :], out_offset=None, in_=xn_rows,
                                        in_offset=bass.IndirectOffsetOnAxis(slot_table[:, i, 0:1], 0)
                                        ).then_inc(gathered[i % 2], 16)

            def scatter(i):
                if i:
                    pool.wait_ge(S["scattered"], i * 16)
                else:
                    pool.wait_ge(S["based"], 16 * B)
                pool.wait_ge(S["y_ready"], i + 1)
                pool.indirect_dma_start(out=a["out"], out_offset=bass.IndirectOffsetOnAxis(slot_table[:, i, 1:2], 0),
                                        in_=yt[:, i % 2, :], in_offset=None, compute_op=ALU.add).then_inc(S["scattered"], 16)

            pool.wait_ge(S["first_rows"], 16)
            pool.wait_ge(S["rows_out"], 16 * B)
            pool.wait_ge(S["routed"], 1)
            gather(0)
            gather(1)
            for i in range(NSLOT):
                if i + 2 < NSLOT:
                    gather(i + 2)
                scatter(i)

        @block.vector
        def _(dve):
            chain = [0]

            def link(ins):
                chain[0] += 1
                ins.then_inc(S["dve_chain"], 1)
                dve.wait_ge(S["dve_chain"], chain[0])

            def row_sums(t0, t1):
                for t in range(t0, t1 - 1):
                    dve.bn_stats(st[:, t, :], x[:, t, :])
                link(dve.bn_stats(st[:, t1 - 1, :], x[:, t1 - 1, :]))

            def variances(t0, t1):
                for t in range(t0, t1 - 1):
                    dve.bn_aggr(mv[:, t, :], st[:, t, :])
                link(dve.bn_aggr(mv[:, t1 - 1, :], st[:, t1 - 1, :]))
                dve.tensor_scalar(sd[:, t0:t1], mv[:, t0:t1, 1], EPS, None, ALU.add).then_inc(S["std_ready"], 1)

            def scale_rows(t):
                dve.tensor_scalar(xn[:, t, :], x[:, t, :], mv[:, t, 0:1], rs[:, t:t + 1],
                                  ALU.subtract, ALU.mult).then_inc(S["ln_done"], 1)

            def reduce_bank(v, c, out):
                piece = MAX_PIECES[c]
                if c == 0 and not (isinstance(v, int) and v == 0):
                    dve.wait_ge(S["m_all"], v)
                if piece[0] == "pair" and not (isinstance(v, int) and v == 0):
                    dve.wait_ge(S["m_split"], v)
                if piece[0] == "cross":
                    m = mx[:, piece[1], piece[2]:piece[2] + 1]
                elif piece[0] == "tail":
                    m, out = mx[:, :, NCH], out[:, 0:TT * TAIL].rearrange("p (q k) -> p q k", q=TT)
                elif piece[0] == "pair":
                    m, out = mneg[:, 0, 0:2], out.rearrange("p (q k) -> p q k", q=2)
                else:
                    m, out = mneg[:, 0, piece[1]:piece[1] + 1], out[:, 0:(piece[1] + 1) * P]
                return dve.tensor_reduce(m, out, AX_X, ALU.max)

            def reduce_piece(v, c):
                dve.wait_ge(S["max_mm"], v * NMAX + (c + 1 - MAXED))
                reduce_bank(v, c, ps[:, 4 + c % 2, :]).then_inc(S["max_red"], 1)

            def max_parts(v, i):
                if i == 0:
                    if not (isinstance(v, int) and v == 0):
                        dve.wait_ge(S["max_red"], v * NMAX + (NMAX - MAXED))
                    dve.tensor_reduce(mneg[:, 1, :], mx[:, :, :], AX_X, ALU.max).then_inc(S["m_all"], 1)
                if i == 1:
                    dve.wait_ge(S["m_all"], v + 1)
                    dve.tensor_scalar(mparts[:, :, :, 0], mneg[:, :, :], -1.0, None, ALU.mult).then_inc(S["m_hi"], 1)
                if i == 2:
                    dve.wait_ge(S["m_hi"], v + 1)
                    dve.scalar_tensor_tensor(out=mparts[:, :, :, 1], in0=mneg[:, :, :], scalar=-1.0,
                                             in1=mparts[:, :, :, 0], op0=ALU.mult, op1=ALU.subtract
                                             ).then_inc(S["m_split"], 1)

            dve.wait_ge(S["early"], EARLY)
            dve.wait_ge(S["pool_chain"], 1)
            for n, p in enumerate(pieces):
                bk = ps[:, n % 7, :]
                b = p[1]
                for later in range(B):
                    ahead, t0 = turn_at[later] - n, later * TT
                    if ahead == LN_SUMS_AT[later]:
                        dve.wait_ge(sequence[later], 48 if later else 16)
                    if 0 <= LN_SUMS_AT[later] - ahead < TT:
                        row_sums(t0 + LN_SUMS_AT[later] - ahead, t0 + LN_SUMS_AT[later] - ahead + 1)
                    if ahead == LN_STD_AT[later]:
                        variances(t0, t0 + TT)
                    if ahead == LN_ROWS_AT[later]:
                        dve.wait_ge(S["sqrt_done"], 1 + later)
                        link(dve.reciprocal(rs[:, t0:t0 + TT], sd[:, t0:t0 + TT]))
                    if 0 <= LN_ROWS_AT[later] - ahead < TT:
                        scale_rows(t0 + LN_ROWS_AT[later] - ahead)
                if n == SETUP:
                    dve.wait_ge(S["loaded"], LOADED)
                    dve.wait_ge(S["masks_load"], MASKS)
                    dve.tensor_copy(maskq[:, :], masks[:, 0:2 * P])
                    dve.tensor_copy(identb[:, :], ident[:, :]).then_inc(S["setup_done"], 1)
                if n == SETUP + 12:
                    dve.wait_ge(S["tanh_done"], 1)
                    dve.tensor_scalar(bv[:, 2, :], bv[:, 2, :], tg[:, 0:1], None, ALU.mult).then_inc(S["bias_gated"], 1)
                dve.wait_ge(S["prep_mm"], n + 1)
                if p[0] == "max":
                    _, v, c = p
                    reduce_bank(v, c, bk).then_inc(S["prep_freed"], 1)
                    if (v, c) == (0, NMAX - 1):
                        dve.wait_ge(S["prep_freed"], n + 1)
                        for i in range(3):
                            max_parts(0, i)
                elif p[0] == "turn":
                    dve.tensor_copy(xnT[:, p[2], b * T:(b + 1) * T], bk).then_inc(S["prep_freed"], 1)
                elif p[0] == "split":
                    _, _, t, hf, c0, c1 = p
                    s = split_of[n]
                    dve.wait_ge(S["hi_done"], s + 1)
                    if s >= NB:
                        dve.wait_ge(S["split_done"], s - NB + 1)
                    dve.scalar_tensor_tensor(out=res[:, s % NB, 0:c1 - c0], in0=bk[:, 0:c1 - c0],
                                             scalar=bqk[:, t, hf:hf + 1], in1=cut[:, s % NB, place_of(t)[0], 0:c1 - c0],
                                             op0=ALU.add, op1=ALU.subtract).then_inc(S["prep_freed"], 1)
                else:
                    t = p[2]
                    kn = CTAIL if t == VT - 1 else P
                    dve.tensor_tensor(v_all[0:kn, b * H:(b + 1) * H, t, :],
                                      bk[0:kn, 0:C].rearrange("p (h d) -> p h d", h=H),
                                      bv[0:kn, 0 if t < TT else 1, :].rearrange("p (h d) -> p h d", h=H),
                                      ALU.add).then_inc(S["prep_freed"], 1)

            def add_rest(u):
                dve.wait_ge(S["o_evac"], u)
                dve.tensor_tensor(osb[0:VW, :], osb[0:VW, :], ps7[P - VW:P, :], ALU.add).then_inc(S["rest_added"], 1)

            def outputs(u, i):
                nm = ps7[:, :].rearrange("p (t q w) -> p t q w", t=TT, q=4)
                if i == 0:
                    dve.wait_ge(S["norm_mm"], u)
                    if not (isinstance(u, int) and u == 1):
                        dve.wait_ge(S["y_parts"], u - 1)
                    dve.tensor_copy(sums[:, 0, :, :], nm[:, :, 3, 0:D + 1])
                    dve.tensor_reduce(sums[:, 1, :, :], nm[:, :, 0:3, 0:D + 1].rearrange("p t q d -> p t d q"),
                                      AX_X, ALU.add).then_inc(S["sums_in"], 1)
                if i == 1:
                    dve.wait_ge(S["sums_in"], u)
                    dve.reciprocal(rsum[:, :, :], sums[:, :, :, D]).then_inc(S["rsum_ready"], 1)

            def step(u, r, prev, nxt, nxt2):
                for c in range(NMAX):
                    if c < HALF and nxt:
                        reduce_piece(u + 1, c + HALF)
                    elif c >= HALF and nxt2:
                        reduce_piece(u + 2, c - HALF)
                    if nxt and HALF - 1 <= c < HALF + 2:
                        max_parts(u + 1, c - HALF + 1)
                    if prev and c == REST_AT:
                        add_rest(u)
                    if prev and OUTPUTS_AT <= c < OUTPUTS_AT + 2:
                        outputs(u, c - OUTPUTS_AT)

            run_steps(dve, step)
            add_rest(NU)
            for i in range(2):
                outputs(NU, i)

            def shared_hidden(tb, it0=0, it1=IT):
                if tb == 1 and it0 == 0:
                    dve.wait_ge(S["rows_out"], 16 * B)
                if tb >= 2:
                    dve.wait_ge(S["down_mm"], tb - 1)
                for it, (i0, m) in [*enumerate(SHARED_CUTS)][it0:it1]:
                    k0 = tb * IT + it
                    dve.wait_ge(S["silu_done"], k0 + 1)
                    up = ps[0:m, 2 * (k0 % 2) + 1, :] if it < WHOLE else ps[m:2 * m, 2 * (k0 % 2), :]
                    dve.tensor_tensor(hT[tb % 2][0:m, it, :], sg[0:m, k0 % 2, :], up,
                                      ALU.mult).then_inc(S["h_done"], 1)

            dve.wait_ge(S["late"], LATE)
            dve.wait_ge(S["y_done"], NU)
            link(dve.memset(wr_cols, 0.0))
            dve.tensor_copy(wr_cols[:, :, 0:NE], wr[:, :, :]).then_inc(S["wr_ready"], 1)

            dve.wait_ge(S["x_biased"], NT)


            def tail_stats(t):
                dve.wait_ge(S["x2_ready"], t + 1)
                if t % TT < TT - 1:
                    dve.bn_stats(st[:, t, :], x[:, t, :])
                else:
                    link(dve.bn_stats(st[:, t, :], x[:, t, :]))
                    variances(t + 1 - TT, t + 1)

            def tail_scale(t):
                if t % TT == 0:
                    dve.wait_ge(S["sqrt_done"], 1 + B + t // TT)
                    link(dve.reciprocal(rs[:, t:t + TT], sd[:, t:t + TT]))
                scale_rows(t)

            for t in range(NT):
                dve.wait_ge(S["proj_mm"], t + 1)
                dve.scalar_tensor_tensor(out=x[:, t, :], in0=ps[:, 4 + t % 3, 0:C], scalar=tg[:, 0:1], in1=x[:, t, :],
                                         op0=ALU.mult, op1=ALU.add).then_inc(S["x2_ready"], 1)
                if t >= 1:
                    tail_stats(t - 1)
                if t >= SCALE_LAG:
                    tail_scale(t - SCALE_LAG)
            tail_stats(NT - 1)
            for t in range(NT - SCALE_LAG, NT):
                tail_scale(t)
            shared_hidden(0)
            shared_hidden(1, 0, 1)
            link(dve.memset(lg[:, :, NE:E8], -3e38))
            dve.wait_ge(S["late"], LATE)
            dve.wait_ge(S["logits_turned"], 1)
            for b in range(B):
                ins = dve.tensor_tensor(lg[:, b * TT:(b + 1) * TT, 0:NE],
                                        ps7.rearrange("p (t b w) -> p t b w", t=TT, b=B)[:, :, b, 0:NE],
                                        rb[:, 0:NE].unsqueeze(1).to_broadcast([P, TT, NE]), ALU.add)
            link(ins)

            def first_largest(src, m, s):
                full = [P, NT, E8]
                link(dve.tensor_reduce(m[:, :], src[:, :, :], AX_X, ALU.max))
                link(dve.tensor_tensor(s[:, :, :], src[:, :, :], m[:, :].unsqueeze(2).to_broadcast(full), ALU.is_equal))
                link(dve.tensor_tensor(key[:, :, :], s[:, :, :], desc[:, :].unsqueeze(1).to_broadcast(full), ALU.mult))
                link(dve.tensor_reduce(km[:, :], key[:, :, :], AX_X, ALU.max))
                link(dve.tensor_tensor(s[:, :, :], key[:, :, :], km[:, :].unsqueeze(2).to_broadcast(full), ALU.is_equal))

            first_largest(lg, m1, s1)
            shared_hidden(1, 1, 2)
            link(dve.scalar_tensor_tensor(out=lg[:, :, :], in0=s1[:, :, :], scalar=-3e38, in1=lg[:, :, :],
                                          op0=ALU.mult, op1=ALU.add))
            first_largest(lg, m2, s2)
            dve.tensor_tensor(took, s1, s2, ALU.add).then_inc(S["took_ready"], 1)
            dve.tensor_tensor(e2[:, :], m2[:, :], m1[:, :], ALU.subtract).then_inc(S["gap_ready"], 1)

            def token_weights():
                dve.wait_ge(S["exp2_done"], 1)
                link(dve.tensor_scalar(rd[:, :], e2[:, :], 1.0, None, ALU.add))
                link(dve.reciprocal(rd[:, :], rd[:, :]))
                link(dve.tensor_scalar(weight[:, 0, :], rd[:, :], tg[:, 1:2], None, ALU.mult))
                link(dve.tensor_tensor(weight[:, 1, :], weight[:, 0, :], e2[:, :], ALU.mult))

            def shared_out(tb):
                dve.wait_ge(S["down_mm"], tb + 1)
                for t in range(TT):
                    n = tb * TT + t
                    ins = dve.scalar_tensor_tensor(out=x[:, n, :], in0=ps[:, 4 + t // 2, (t % 2) * C:(t % 2 + 1) * C],
                                                   scalar=tg[:, 1:2], in1=x[:, n, :], op0=ALU.mult, op1=ALU.add)
                ins.then_inc(S["acc_done"], 1)

            def first_slots():
                link(dve.memset(running[:, :, 0:LEAD, :], 0.0))
                dve.wait_ge(S["counts_out"], 1)
                steps = [1 << i for i in range((NT - 1).bit_length())]
                for i, d in enumerate(steps):
                    old, new = running[:, i % 2], running[:, 1 - i % 2]
                    link(dve.tensor_tensor(new[:, LEAD:, :], old[:, LEAD:, :], old[:, LEAD - d:LEAD - d + NT, :], ALU.add))
                sums_to = running[:, len(steps) % 2]
                link(dve.tensor_tensor(counts, sums_to[:, LEAD - 1:LEAD - 1 + NT, :],
                                       ps[:, 6, 0:NT * E8].rearrange("p (t e) -> p t e", t=NT), ALU.add))
                dve.wait_ge(S["route_load"], 16)
                full = [P, E8, NT]
                link(dve.tensor_tensor(passed, sums_to[:, LEAD + NT - 1, :].unsqueeze(2).to_broadcast(full),
                                       bounds.unsqueeze(1).to_broadcast(full), ALU.is_gt))
                link(dve.tensor_reduce(ntiles, passed, AX_X, ALU.add))
                link(dve.tensor_tensor(earlier, ntiles.unsqueeze(1).to_broadcast([P, E8, E8]),
                                       below.rearrange("p (a b) -> p a b", a=E8), ALU.mult))
                link(dve.tensor_reduce(start, earlier, AX_X, ALU.add))
                full = [P, NSLOT, NE - 1]
                link(dve.tensor_tensor(reached, tile_no.unsqueeze(2).to_broadcast(full),
                                       start[:, 1:NE].unsqueeze(1).to_broadcast(full), ALU.is_ge))
                link(dve.tensor_reduce(expert_no, reached, AX_X, ALU.add))
                link(dve.tensor_copy(tile_expert[:, :], expert_no))
                link(dve.tensor_scalar(start, start, float(P), None, ALU.mult))
                link(dve.tensor_tensor(at, counts, start.unsqueeze(1).to_broadcast([P, NT, E8]), ALU.add))
                for k, s in enumerate((s1, s2)):
                    link(dve.tensor_tensor(taken, s, at, ALU.mult))
                    link(dve.tensor_reduce(slot[:, k, :], taken, AX_X, ALU.add))

            def table_parts(k):
                full = [P, NT, NSLOT + 1]
                link(dve.tensor_tensor(from_tile, slot[:, k, :].unsqueeze(2).to_broadcast(full),
                                       tile_begin.unsqueeze(1).to_broadcast(full), ALU.is_ge))
                link(dve.tensor_reduce(slot_tile[:, k, :], from_tile[:, :, 1:NSLOT + 1], AX_X, ALU.add))
                link(dve.scalar_tensor_tensor(out=lane[:, k, :], in0=slot_tile[:, k, :], scalar=-float(P), in1=slot[:, k, :],
                                              op0=ALU.mult, op1=ALU.add))
                if k:
                    dve.wait_ge(S["table_mm"], 4)
                full = [P, NT, NSLOT]
                link(dve.tensor_tensor(row_in[:, :, NSLOT:2 * NSLOT], from_tile[:, :, 0:NSLOT], from_tile[:, :, 1:NSLOT + 1],
                                       ALU.subtract))
                link(dve.tensor_tensor(row_in[:, :, 0:NSLOT], row_in[:, :, NSLOT:2 * NSLOT],
                                       token_no.unsqueeze(2).to_broadcast(full), ALU.mult))
                link(dve.tensor_tensor(row_in[:, :, NSLOT:2 * NSLOT], row_in[:, :, NSLOT:2 * NSLOT],
                                       weight[:, k, :].unsqueeze(2).to_broadcast(full), ALU.mult))

            def table_lanes(k, n0, n1):
                full = [P, 4, P]
                for n in range(n0, n1):
                    g = 4 * k + n
                    if g >= 2:
                        dve.wait_ge(S["table_mm"], g - 1)
                    dve.tensor_tensor(in_lane[:, g % 2], slot_of.unsqueeze(1).to_broadcast(full),
                                      lane[:, k, 4 * n:4 * n + 4].unsqueeze(2).to_broadcast(full), ALU.is_equal
                                      ).then_inc(S["lane_ready"], 1)

            def finish_table():
                dve.wait_ge(S["table_out"], 1)
                link(dve.tensor_scalar(empty, table, 0.0, spare_row, ALU.is_equal, ALU.mult))
                link(dve.scalar_tensor_tensor(out=result_at, in0=table, scalar=-1.0, in1=empty, op0=ALU.add, op1=ALU.add))
                link(dve.tensor_copy(slot_table[:, :, 1], result_at))
                link(dve.tensor_scalar(back, result_at, float(NTOK), -float(NTOK), ALU.is_ge, ALU.mult))
                link(dve.tensor_tensor(back, result_at, back, ALU.add))
                dve.tensor_copy(slot_table[:, :, 0], back).then_inc(S["routed"], 1)

            def rows_turned(i, b, bank=5):
                dve.wait_ge(S["turned"], i + 1)
                dve.tensor_copy(xgT[:, b, :, :].rearrange("p k t -> p (k t)"), ps[:, bank, 0:2 * P]).then_inc(S["xT_ready"], 1)

            def hidden(i):
                for c in range(2):
                    dve.wait_ge(S["silu2_done"], i * 2 + (c + 1))
                    dve.tensor_tensor(hid[:, c, :], gate_s[:, c, :], ps[:, 2 * c + 1, 0:CH], ALU.mult).then_inc(S["h2_done"], 1)

            def result(i, b, first):
                if not first:
                    dve.wait_ge(S["scattered"], i * 16 - 16)
                dve.wait_ge(S["down2_mm"], i + 1)
                dve.tensor_scalar(yt[:, b, :], ps[:, 4, 0:C], slot_weight[:, bass.ds(i, 1)], None, ALU.mult
                                  ).then_inc(S["y_ready"], 1)

            def turn(i, b, first):
                hidden(i)
                rows_turned(i + 1, 1 - b)
                result(i - 1, 1 - b, first)

            shared_hidden(1, 2, IT)
            token_weights()
            first_slots()
            table_parts(0)
            table_lanes(0, 0, 2)
            shared_out(0)
            shared_hidden(2)
            table_lanes(0, 2, 4)
            table_parts(1)
            table_lanes(1, 0, 2)
            shared_out(1)
            shared_hidden(3)
            table_lanes(1, 2, 4)
            finish_table()
            shared_out(2)
            rows_turned(0, 0, bank=6)
            shared_out(3)
            hidden(0)
            rows_turned(1, 1)
            turn(1, 1, True)
            turn(2, 0, True)
            with dve.Fori(1, NSLOT // 2 - 1) as i:
                turn(i * 2 + 1, 1, False)
                turn(i * 2 + 2, 0, False)
            hidden(NSLOT - 1)
            result(NSLOT - 2, 0, False)
            result(NSLOT - 1, 1, False)


def kernel(**inputs):
    import numpy as np
    import concourse.bacc as bacc
    from concourse.bass_utils import run_bass_kernel_spmd

    i = {k.replace("L0_xattn_", "").replace("L0_ffn_", ""): np.asarray(v) for k, v in inputs.items()}

    def over(v, n):
        return np.broadcast_to(v.reshape(1, n), (P, n))

    future = np.triu(np.full((P, P), LOW, np.float32), 1)
    masks = np.concatenate([future, np.full((P, P), LOW, np.float32)], axis=1)
    lane = np.arange(P).reshape(P, 1)
    tokens = np.arange(NT).reshape(1, NT) * P + lane
    route = np.concatenate([np.triu(np.ones((P, P)), 1), np.ones((P, P)), over(np.arange(P), P), over(np.arange(NT) * P, NT),
                            over(np.tril(np.ones((E8, E8)), -1), E8 * E8), over(np.arange(NSLOT), NSLOT),
                            over(np.arange(NSLOT + 1) * P, NSLOT + 1), tokens + 1, NTOK + lane + 1],
                           axis=1).astype(np.float32)

    def expert_weights(g, u, d, cuts):
        dn = np.zeros((P, IT, C), np.float32)
        for it, (i0, m) in enumerate(cuts):
            dn[:m, it] = d.T[i0:i0 + m]
        gate, up = [w.T.reshape(2, P, I).transpose(1, 0, 2) for w in (g, u)]
        if cuts is CUTS:
            ups = [gate.reshape(P, 2 * I), up.reshape(P, 2 * I)]
        else:
            ups = [np.concatenate([gate, up[:, :, WHOLE * P:], up[:, :, :WHOLE * P]], axis=2).reshape(P, 4 * I)]
        return np.concatenate(ups + [dn.reshape(P, IT * C)], axis=1)

    experts = [expert_weights(i["rg"][e], i["ru"][e], i["rd"][e], CUTS) for e in range(NE)]
    experts.append(expert_weights(i["sg"], i["su"], i["sd"], SHARED_CUTS))
    arrays = {
        "x": i["x"].reshape(B * T, C),
        "ctxT": i["ctx_512"].transpose(2, 0, 1).reshape(CC, B * TC),
        "Wq": i["Wq"], "Wcq": i["Wcq"], "Wk": i["Wk"], "Wck": i["Wck"], "Wv": i["Wv"], "Wcv": i["Wcv"], "Wp": i["Wp"],
        "bqk": np.stack([i[n].reshape(2, P).T for n in ("bq", "bcq", "bk", "bck")], axis=1),
        "bvp": np.stack([over(i[n], C) for n in ("bv", "bcv", "bp")], axis=1),
        "gates": np.concatenate([over(i["g_xattn"], 1), over(i["g_ffn"], 1)], axis=1),
        "wrT": i["wr"].T,
        "rb": np.concatenate([over(i["rb"], NE), np.zeros((P, 1), np.float32)], axis=1),
        "experts": np.stack(experts), "route": route,
        "ident": np.eye(P, dtype=np.float32), "masks": masks,
        "desc": over(np.arange(E8, 0, -1).astype(np.float32), E8),
    }
    arrays = {k: np.ascontiguousarray(v) for k, v in arrays.items()}
    nc = bacc.Bacc("TRN2", target_bir_lowering=False, num_devices=1)
    aps = {k: nc.dram_tensor("in_" + k, v.shape, F32, kind="ExternalInput").ap() for k, v in arrays.items()}
    aps["out"] = nc.dram_tensor("out", (NTOK + P, C), F32, kind="ExternalOutput").ap()
    program(nc, aps)
    r = run_bass_kernel_spmd(nc, [{"in_" + k: v for k, v in arrays.items()}], core_ids=[0])
    return r.results[0]["out"][0:NTOK].reshape(B, T, C)
```
